# Optimizing a Trainium2 kernel written in Bass

```python
import numpy as np
import jax
import jax.numpy as jnp

def _softmax(x, axis=-1):
    return jax.nn.softmax(x, axis=axis)

def _gelu(x):
    return jax.nn.gelu(x, approximate=True)

def _silu(x):
    return jax.nn.silu(x)

def _sigmoid(x):
    return jax.nn.sigmoid(x)

def _layernorm(x, axis=-1, eps=1e-05):
    m = jnp.mean(x, axis=axis, keepdims=True)
    v = jnp.var(x, axis=axis, keepdims=True)
    return (x - m) / jnp.sqrt(v + eps)

def _scatter_add(tgt, idx, src, axis=0):
    return tgt.at[idx].add(src)

def _segment_sum(src, seg, n):
    return jax.ops.segment_sum(src, seg, n)
kernel_name = 'mk_seq_preln_d1_jaxref_r8_e559d8'

def setup_inputs(seed: int=0):
    np.random.seed(seed)
    _w = jnp.asarray

    def _L0_attn_setup():
        import jax, jax.numpy as jnp
        import numpy as np
        B, S, H = (16, 64, 256)
        NH, NKV = (16, 4)
        HD = H // NH

        def _rope_tables(seq_len, dim, dtype):
            inv_freq = 1.0 / 10000.0 ** (jnp.arange(0, dim, 2, dtype=jnp.float32) / dim)
            t = jnp.arange(seq_len, dtype=jnp.float32)
            freqs = jnp.einsum('i,j->ij', t, inv_freq)
            emb = jnp.concatenate([freqs, freqs], axis=-1)
            cos = jnp.cos(emb)[None, None].astype(dtype)
            sin = jnp.sin(emb)[None, None].astype(dtype)
            return (cos, sin)

        def _rotate_half(x):
            x1, x2 = jnp.split(x, 2, axis=-1)
            return jnp.concatenate([-x2, x1], axis=-1)
        key = jax.random.key(seed)
        kx, kq, kk, kv, ko = jax.random.split(key, 5)
        x = jax.random.normal(kx, (B, S, H), dtype=jnp.float32)
        s = 0.02
        Wq = jax.random.normal(kq, (H, H), dtype=jnp.float32) * s
        Wk = jax.random.normal(kk, (NKV * HD, H), dtype=jnp.float32) * s
        Wv = jax.random.normal(kv, (NKV * HD, H), dtype=jnp.float32) * s
        Wo = jax.random.normal(ko, (H, H), dtype=jnp.float32) * s
        return {'x': x, 'Wq': Wq, 'Wk': Wk, 'Wv': Wv, 'Wo': Wo}
    _L0_attn_in = _L0_attn_setup()

    def _L0_ffn_setup():
        import jax, jax.numpy as jnp
        import numpy as np
        B, S, H = (1, 128, 256)
        I = 176
        E = 32
        K = 6
        G = 8
        TG = 3
        NSH = 2
        SCALE = 16.0
        C = 48

        def _moe_forward(x3, gate_w, w_gate_up, w_down, ws_gate_up, ws_down):
            b, s, h = x3.shape
            x = x3.reshape(-1, h)
            T = x.shape[0]
            logits = x @ gate_w.T
            grouped = logits.reshape(T, G, E // G)
            group_scores = jnp.max(grouped, axis=-1)
            _, group_idx = jax.lax.top_k(group_scores, TG)
            group_keep = jnp.zeros((T, G), bool).at[jnp.arange(T)[:, None], group_idx].set(True)
            masked = jnp.where(group_keep[..., None], grouped, 0.0)
            scores = masked.reshape(T, E)
            probs = jax.nn.softmax(scores.astype(jnp.float32), axis=-1)
            topk_w, topk_idx = jax.lax.top_k(probs, K)
            topk_w = topk_w * SCALE
            flat_e = topk_idx.reshape(-1)
            tok_idx = jnp.repeat(jnp.arange(T), K)
            oh = jax.nn.one_hot(flat_e, E, dtype=jnp.int32)
            pos = jnp.take_along_axis(jnp.cumsum(oh, axis=0) - 1, flat_e[:, None], axis=1)[:, 0]
            valid = pos < C
            slot = jnp.where(valid, flat_e * C + pos, E * C)
            buf = jnp.zeros((E * C + 1, h), x.dtype).at[slot].set(x[tok_idx])
            xb = buf[:E * C].reshape(E, C, h)
            gu = jnp.einsum('ech,ehf->ecf', xb, w_gate_up)
            g, u = jnp.split(gu, 2, axis=-1)
            act = jax.nn.silu(g) * u
            yb = jnp.einsum('eci,eih->ech', act, w_down)
            yflat = jnp.concatenate([yb.reshape(E * C, h), jnp.zeros((1, h), yb.dtype)], axis=0)
            y_pairs = yflat[slot].reshape(T, K, h)
            out = jnp.einsum('tk,tkh->th', topk_w.astype(x.dtype), y_pairs)
            gu_s = x @ ws_gate_up
            gs, us = jnp.split(gu_s, 2, axis=-1)
            out = out + jax.nn.silu(gs) * us @ ws_down
            return out.reshape(b, s, h)
        key = jax.random.key(seed)
        ks = jax.random.split(key, 6)
        s = 0.02
        return {'hidden_states': jax.random.normal(ks[0], (B, S, H), jnp.float32), 'gate_w': jax.random.normal(ks[1], (E, H), jnp.float32) * s, 'w_gate_up': jax.random.normal(ks[2], (E, H, 2 * I), jnp.float32) * s, 'w_down': jax.random.normal(ks[3], (E, I, H), jnp.float32) * s, 'ws_gate_up': jax.random.normal(ks[4], (H, 2 * I * NSH), jnp.float32) * s, 'ws_down': jax.random.normal(ks[5], (I * NSH, H), jnp.float32) * s}
    _L0_ffn_in = _L0_ffn_setup()
    _d = {'L0_attn_x': _L0_attn_in['x'], 'L0_attn_Wq': _L0_attn_in['Wq'], 'L0_attn_Wk': _L0_attn_in['Wk'], 'L0_attn_Wv': _L0_attn_in['Wv'], 'L0_attn_Wo': _L0_attn_in['Wo'], 'L0_ffn_gate_w': _L0_ffn_in['gate_w'], 'L0_ffn_w_gate_up': _L0_ffn_in['w_gate_up'], 'L0_ffn_w_down': _L0_ffn_in['w_down'], 'L0_ffn_ws_gate_up': _L0_ffn_in['ws_gate_up'], 'L0_ffn_ws_down': _L0_ffn_in['ws_down']}
    _x0 = _d['L0_attn_x']
    _d['L0_attn_x'] = jax.random.normal(jax.random.fold_in(jax.random.key(seed), 1), (4, 512, 256), dtype=_x0.dtype)
    del _x0
    return _d

def reference(L0_attn_x, L0_attn_Wq, L0_attn_Wk, L0_attn_Wv, L0_attn_Wo, L0_ffn_gate_w, L0_ffn_w_gate_up, L0_ffn_w_down, L0_ffn_ws_gate_up, L0_ffn_ws_down):

    def _L0_attn_ref(x, Wq, Wk, Wv, Wo):
        import jax, jax.numpy as jnp
        import numpy as np
        B, S, H = (16, 64, 256)
        NH, NKV = (16, 4)
        HD = H // NH

        def _rope_tables(seq_len, dim, dtype):
            inv_freq = 1.0 / 10000.0 ** (jnp.arange(0, dim, 2, dtype=jnp.float32) / dim)
            t = jnp.arange(seq_len, dtype=jnp.float32)
            freqs = jnp.einsum('i,j->ij', t, inv_freq)
            emb = jnp.concatenate([freqs, freqs], axis=-1)
            cos = jnp.cos(emb)[None, None].astype(dtype)
            sin = jnp.sin(emb)[None, None].astype(dtype)
            return (cos, sin)

        def _rotate_half(x):
            x1, x2 = jnp.split(x, 2, axis=-1)
            return jnp.concatenate([-x2, x1], axis=-1)
        b, s, _ = x.shape
        scaling = HD ** (-0.5)
        q = jnp.einsum('bsh,oh->bso', x, Wq).reshape(b, s, NH, HD).transpose(0, 2, 1, 3)
        k = jnp.einsum('bsh,oh->bso', x, Wk).reshape(b, s, NKV, HD).transpose(0, 2, 1, 3)
        v = jnp.einsum('bsh,oh->bso', x, Wv).reshape(b, s, NKV, HD).transpose(0, 2, 1, 3)
        cos, sin = _rope_tables(s, HD, x.dtype)
        q = q * cos + _rotate_half(q) * sin
        k = k * cos + _rotate_half(k) * sin
        rep = NH // NKV
        k = jnp.repeat(k, rep, axis=1)
        v = jnp.repeat(v, rep, axis=1)
        scores = jnp.einsum('bhqd,bhkd->bhqk', q, k) * scaling
        attn = jax.nn.softmax(scores, axis=-1)
        out = jnp.einsum('bhqk,bhkd->bhqd', attn, v)
        out = out.transpose(0, 2, 1, 3).reshape(b, s, H)
        return jnp.einsum('bsh,oh->bso', out, Wo)

    def _L0_ffn_ref(hidden_states, gate_w, w_gate_up, w_down, ws_gate_up, ws_down):
        import jax, jax.numpy as jnp
        import numpy as np
        B, S, H = (1, 128, 256)
        I = 176
        E = 32
        K = 6
        G = 8
        TG = 3
        NSH = 2
        SCALE = 16.0
        C = 48

        def _moe_forward(x3, gate_w, w_gate_up, w_down, ws_gate_up, ws_down):
            b, s, h = x3.shape
            x = x3.reshape(-1, h)
            T = x.shape[0]
            logits = x @ gate_w.T
            grouped = logits.reshape(T, G, E // G)
            group_scores = jnp.max(grouped, axis=-1)
            _, group_idx = jax.lax.top_k(group_scores, TG)
            group_keep = jnp.zeros((T, G), bool).at[jnp.arange(T)[:, None], group_idx].set(True)
            masked = jnp.where(group_keep[..., None], grouped, 0.0)
            scores = masked.reshape(T, E)
            probs = jax.nn.softmax(scores.astype(jnp.float32), axis=-1)
            topk_w, topk_idx = jax.lax.top_k(probs, K)
            topk_w = topk_w * SCALE
            flat_e = topk_idx.reshape(-1)
            tok_idx = jnp.repeat(jnp.arange(T), K)
            oh = jax.nn.one_hot(flat_e, E, dtype=jnp.int32)
            pos = jnp.take_along_axis(jnp.cumsum(oh, axis=0) - 1, flat_e[:, None], axis=1)[:, 0]
            valid = pos < C
            slot = jnp.where(valid, flat_e * C + pos, E * C)
            buf = jnp.zeros((E * C + 1, h), x.dtype).at[slot].set(x[tok_idx])
            xb = buf[:E * C].reshape(E, C, h)
            gu = jnp.einsum('ech,ehf->ecf', xb, w_gate_up)
            g, u = jnp.split(gu, 2, axis=-1)
            act = jax.nn.silu(g) * u
            yb = jnp.einsum('eci,eih->ech', act, w_down)
            yflat = jnp.concatenate([yb.reshape(E * C, h), jnp.zeros((1, h), yb.dtype)], axis=0)
            y_pairs = yflat[slot].reshape(T, K, h)
            out = jnp.einsum('tk,tkh->th', topk_w.astype(x.dtype), y_pairs)
            gu_s = x @ ws_gate_up
            gs, us = jnp.split(gu_s, 2, axis=-1)
            out = out + jax.nn.silu(gs) * us @ ws_down
            return out.reshape(b, s, h)
        return _moe_forward(hidden_states, gate_w, w_gate_up, w_down, ws_gate_up, ws_down)
    x = L0_attn_x
    x = x + _L0_attn_ref(_layernorm(x, axis=-1), L0_attn_Wq, L0_attn_Wk, L0_attn_Wv, L0_attn_Wo)
    x = x + _L0_ffn_ref(_layernorm(x, axis=-1), L0_ffn_gate_w, L0_ffn_w_gate_up, L0_ffn_w_down, L0_ffn_ws_gate_up, L0_ffn_ws_down)
    return x

_drawn_inputs = setup_inputs


def setup_inputs(seed=0):
    import zlib

    import numpy as np

    out = dict(_drawn_inputs(seed))
    spreads = {}
    factors = {'L0_attn_Wq': 8.0,
     'L0_attn_Wk': 8.0,
     'L0_attn_Wv': 8.0,
     'L0_attn_Wo': 8.0,
     'L0_ffn_gate_w': 24.984,
     'L0_ffn_ws_gate_up': 14.654,
     'L0_ffn_ws_down': 14.639,
     'L0_ffn_w_gate_up': 8.0,
     'L0_ffn_w_down': 8.0}
    for name, (base, spread) in spreads.items():
        noise = np.random.default_rng([zlib.crc32(name.encode()), seed]).standard_normal(out[name].shape)
        drawn = base * np.exp(spread * noise) if base else spread * noise
        out[name] = jnp.asarray(drawn.astype(out[name].dtype))
    for name, factor in factors.items():
        out[name] = (out[name] * factor).astype(out[name].dtype)
    return out
```

```python
from contextlib import ExitStack

import concourse.bass as bass
from concourse import mybir

F32 = mybir.dt.float32
BF16 = mybir.dt.bfloat16
U32 = mybir.dt.uint32
ALU = mybir.AluOpType
ACT = mybir.ActivationFunctionType
AX = mybir.AxisListType

P = 128
NB, S, H = 4, 512, 256
T = NB * S
NT = S // P
HK = H // P
NH, NKV = 16, 4
HD = H // NH
REP = NH // NKV
E, I, TOPK, C = 32, 176, 6, 48
G, TG = 8, 3
EG = E // G
ISH = 2 * I
SCALE_W = 16.0
EPS = 1e-5
ATT_SCALE = float(HD) ** -0.5
PAIRS = E // 2
ROWS = T + P
XW = H + E
MROW = 96
KR = 99
QPART = (0, 0, 1, 1, 0, 2)
KPART = (0, 1, 0, 1, 2, 0)

STEPS = NB * NKV
UNITS = STEPS * 16
LAG = 22
AVLAG = LAG + 6
NP, NS = 3, 3
END = 16 * (STEPS + 4)

PRE = {(0, 4): "T0", (0, 5): "T1", (0, 8): "Q0", (0, 15): "Q1", (1, 6): "KV", (1, 9): "VT"}
POST = {(1, 12): "W0", (1, 14): "W1", (2, 3): "U0", (2, 4): "U1", (2, 6): "GL", (2, 8): "GT",
        (2, 10): "A0", (2, 11): "A1", (2, 14): "A2", (2, 15): "A3", (3, 2): "A4", (3, 3): "A5",
        (3, 6): "ST", (3, 9): "D0", (3, 12): "D1"}
PROLOGUE = ["T0", "T1", "Q0", "Q1", "KV", "VT"]


def products_at(t):
    b, r, u = t // 64, t // 16 % 4, t % 16
    out = []
    if u == 0 and 1 <= t // 16 <= STEPS:
        out.append(("MT", t // 16 - 1))
    if (r, u) in PRE and b + 1 < NB:
        out.append((PRE[r, u], b + 1))
    if (r, u) in POST and 1 <= b <= NB:
        out.append((POST[r, u], b - 1))
    return out


ORDER = [(n, 0) for n in PROLOGUE] + [p for t in range(END) for p in products_at(t)]
PLACE = {p: n for n, p in enumerate(ORDER)}


def norms_at(t):
    out = [(0, t // 64 + 1)] if t % 64 == 0 and 0 <= t and t // 64 + 1 < NB else []
    return out + ([(1, t // 64 - 1)] if t % 64 == 32 and t >= 64 and t // 64 - 1 < NB else [])


NORMS = [(0, 0)] + [n for t in range(END) for n in norms_at(t)]
NORM_AT = {n: i + 1 for i, n in enumerate(NORMS)}


def moe_kernel(nc, x, wq, wkv, wo, gate, wsgu, wsd, wgu, wd, cosr, sinr, ident_in, keys_in, tri_in,
               emask_in, pad_in, out):
    x_scr = nc.dram_tensor("x_scr", [ROWS, XW], F32).ap()
    plane = nc.dram_tensor("plane", [2 * ROWS, H], F32).ap()
    q_scr = nc.dram_tensor("q_scr", [2, 3, H, S], BF16).ap()
    k_scr = nc.dram_tensor("k_scr", [2, 3, NKV * HD, S], BF16).ap()

    with ExitStack() as ctx:
        def sb(name, shape, dt=F32):
            return ctx.enter_context(nc.sbuf_tensor(name, shape, dt))

        def sem(name):
            return ctx.enter_context(nc.semaphore(name))

        ps_a = ctx.enter_context(nc.psum_tensor("ps_a", [P, 1, S], F32))
        ps_a2 = ctx.enter_context(nc.psum_tensor("ps_a2", [P, 1, S], F32))
        ps_s = ctx.enter_context(nc.psum_tensor("ps_s", [P, NS, S], F32))
        ps_o = ctx.enter_context(nc.psum_tensor("ps_o", [P, 1, S], F32))
        ps_m = ctx.enter_context(nc.psum_tensor("ps_m", [P, 2, S], F32))
        score = [ps_a, ps_a2]

        xs = sb("xs", [P, NB * NT, H])
        wq_s, wkv_s = sb("wq_s", [P, HK, H]), sb("wkv_s", [P, HK, P])
        wo_s, gate_s = sb("wo_s", [P, NKV, H]), sb("gate_s", [P, HK, E])
        wsgu_s, wsd_s = sb("wsgu_s", [P, HK, 2 * ISH]), sb("wsd_s", [P, 3, H])
        cos_s, sin_s = sb("cos_s", [P, S]), sb("sin_s", [P, S])
        ident, keys = sb("ident", [P, P]), sb("keys", [P, NB, P])
        tri, emask, pad = sb("tri", [P, G, G]), sb("emask", [P, PAIRS, E]), sb("pad", [P, 2])
        xn, xr = sb("xn", [P, NT, H]), sb("xr", [P, NT, XW])
        xt, xrt = sb("xt", [P, HK, S]), sb("xrt", [P, HK, S])
        qa, qb = sb("qa", [P, 3, S]), sb("qb", [P, 3, S])
        part = sb("part", [P, 3, 3, S], BF16)
        vt, vs = sb("vt", [P, S]), sb("vs", [P, 2, NT, NKV, 2 * HD])
        ot, rec, recs = sb("ot", [P, NKV, S]), sb("rec", [P, S]), sb("recs", [P, S])
        hs, th = sb("hs", [P, 3, S]), sb("th", [P, S])
        mx, mr, mrow = sb("mx", [P, 2, 16]), sb("mr", [16, P]), sb("mrow", [16, 2, 3, P], BF16)
        stat, agg = sb("stat", [P, 2, NT, 6]), sb("agg", [P, 2, NT, 2])
        rstd, halfs = sb("rstd", [P, 2, NT]), sb("halfs", [P, NT])
        lgt, lg = sb("lgt", [P, P]), sb("lg", [P, NT, E])
        gs, cmp, eq = sb("gs", [P, NT, G]), sb("cmp", [P, NT, G, G]), sb("eq", [P, NT, G, G])
        rank, ex, exs = sb("rank", [P, NT, G]), sb("ex", [P, NT, E]), sb("exs", [P, NT, 4])
        top, rep, sel = sb("top", [P, NT, 8]), sb("rep", [P, NT, E]), sb("sel", [P, NT, E])
        cand, best = sb("cand", [P, C + P]), sb("best", [P, C])
        merged, best2 = sb("merged", [E, 4 * C]), sb("best2", [E, 64])
        idf, idz, idx = sb("idf", [P, 16]), sb("idz", [P, 16]), sb("idx", [P, 2, 16], U32)
        wslot, wtmp = sb("wslot", [P, PAIRS]), sb("wtmp", [P, PAIRS, E])
        zero = sb("zero", [P, XW])

        QSB, KSB, PTB = 2 * NH * S // 2, 2 * NKV * S // 2, NP * REP * S
        big = sb("big", [P, QSB + KSB + PTB])
        qs = big[:, 0:QSB].bitcast(BF16).rearrange("p (b h s) -> p b h s", b=2, h=NH)
        ks = big[:, QSB:QSB + KSB].bitcast(BF16).rearrange("p (b h s) -> p b h s", b=2, h=NKV)
        pt = big[:, QSB + KSB:].rearrange("p (n h s) -> p n h s", n=NP, h=REP)
        EWG, EWD = HK * 2 * I, 2 * H
        NPRE = 4
        NRING = 6
        ew = [sb(f"ew{n}", [P, EWG + EWD]) for n in range(NPRE)]
        ew += [big[:, n * (EWG + EWD):(n + 1) * (EWG + EWD)] for n in range(NRING)]
        at0 = NRING * (EWG + EWD)
        xg = big[:, at0:at0 + PAIRS * XW].rearrange("p (j w) -> p j w", j=PAIRS)
        at0 += PAIRS * XW
        xgt = big[:, at0:at0 + 2 * H].rearrange("p (n k c) -> p n k c", n=2, k=HK)
        at0 += 2 * H
        egu = big[:, at0:at0 + 4 * I].rearrange("p (n f) -> p n f", n=4)
        at0 += 4 * I
        eat = big[:, at0:at0 + 2 * H].rearrange("p (n k c) -> p n k c", n=2, k=2)
        at0 += 2 * H
        ey = big[:, at0:at0 + 2 * H].rearrange("p (n o) -> p n o", n=2)
        at0 += 2 * H
        fin = big[:, at0:at0 + 8 * H].rearrange("p (n a i o) -> p n a i o", n=2, a=2, i=2)
        at0 += 8 * H
        assert at0 <= QSB + KSB + PTB, (at0, QSB + KSB + PTB)

        d_x = [sem(f"d_x{b}") for b in range(NB)]
        d_c0, d_c1 = sem("d_c0"), sem("d_c1")
        d_wqkv, d_wsh = sem("d_wqkv"), sem("d_wsh")
        d_ew = [sem(f"d_ew{n}") for n in range(NPRE + NRING)]
        d_part = [sem("d_part0"), sem("d_part1")]
        d_stack = [sem("d_stack0"), sem("d_stack1")]
        d_mrow = [sem("d_mrow0"), sem("d_mrow1")]
        d_scr, d_zero, d_merge = sem("d_scr"), sem("d_zero"), sem("d_merge")
        d_gather, d_plane = sem("d_gather"), sem("d_plane")
        d_fin, d_out = [sem("d_fin0"), sem("d_fin1")], sem("d_out")
        s_const, s_dve, s_pool = sem("s_const"), sem("s_dve"), sem("s_pool")
        s_p1, s_max = sem("s_p1"), sem("s_max")
        s_p2, s_exp = sem("s_p2"), sem("s_exp")
        s_av, s_norm = sem("s_av"), sem("s_norm")
        m_full = [sem("m_full0"), sem("m_full1")]
        m_taken = [sem("m_taken0"), sem("m_taken1")]
        s_var, s_rstd, s_xn = sem("s_var"), sem("s_rstd"), sem("s_xn")
        s_v, s_roped = sem("s_v"), sem("s_roped")
        s_hi, s_res, s_mid, s_lo = sem("s_hi"), sem("s_res"), sem("s_mid"), sem("s_lo")
        s_mrow, s_tanh = sem("s_mrow"), sem("s_tanh")
        s_mask, s_ex, s_sel, s_row = sem("s_mask"), sem("s_ex"), sem("s_sel"), sem("s_row")
        s_best, s_tk, s_idp, s_idx, s_ws = sem("s_best"), sem("s_tk"), sem("s_idp"), sem("s_idx"), sem("s_ws")
        s_pad, s_fin = sem("s_pad"), sem("s_fin")
        e_xt, e_xtc, e_gu, e_th = sem("e_xt"), sem("e_xtc"), sem("e_gu"), sem("e_th")
        e_act, e_at, e_atc, e_dn, e_y = sem("e_act"), sem("e_at"), sem("e_atc"), sem("e_dn"), sem("e_y")
        RING = [(e % (NPRE + NRING), e // (NPRE + NRING)) for e in range(E)]

        def bank(p):
            return ps_m[:, PLACE[p] % 2, :]

        def wait_bank(eng, p):
            n = PLACE[p]
            if n >= 2:
                eng.wait_ge(m_taken[n % 2], n // 2)

        def wait_product(eng, p):
            eng.wait_ge(m_full[PLACE[p] % 2], PLACE[p] // 2 + 1)

        def full(p):
            return m_full[PLACE[p] % 2]

        def taken(p):
            return m_taken[PLACE[p] % 2]

        def wait_taken(eng, p):
            eng.wait_ge(m_taken[PLACE[p] % 2], PLACE[p] // 2 + 1)

        block = ctx.enter_context(nc.Block())

        @block.sync
        def _(sp):
            for b in range(NB):
                sp.dma_start(xs[:, NT * b:NT * b + NT, :],
                             x[S * b:S * b + S, :].rearrange("(i p) h -> p i h", p=P)).then_inc(d_x[b], 16)
                if b == 0:
                    sp.dma_start(ident[:, :], ident_in).then_inc(d_c0, 16)
                    sp.dma_start(wq_s[:, :, :], wq.rearrange("(k p) o -> p k o", p=P)).then_inc(d_wqkv, 16)
                    sp.dma_start(wkv_s[:, :, :], wkv.rearrange("(k p) o -> p k o", p=P)).then_inc(d_wqkv, 16)
                    sp.dma_start(cos_s[:, :], cosr).then_inc(d_c0, 16)
                    sp.dma_start(sin_s[:, :], sinr).then_inc(d_c0, 16)

            def stack_out(b):
                q = b % 2
                sp.wait_ge(s_lo, 3 * (b + 1))
                if b >= 2:
                    sp.wait_ge(d_stack[q], 16 * 12 * (b // 2))
                for j in range(3):
                    for m in range(2):
                        sp.dma_start(q_scr[q, j, P * m:P * m + P, :], part[:, j, m, :]).then_inc(d_part[q], 16)
                    sp.dma_start(k_scr[q, j, :, :], part[0:NKV * HD, j, 2, :]).then_inc(d_part[q], 16)

            def stack_in(b):
                q = b % 2
                sp.wait_ge(d_part[q], 16 * 9 * (b // 2 + 1))
                if b >= 2:
                    sp.wait_ge(s_p2, 64 * (b - 1))
                for r in range(6):
                    sp.dma_start(qs[16 * r:16 * r + 16, q, :, :],
                                 q_scr[q, QPART[r]].rearrange("(h d) s -> d h s", d=HD)).then_inc(d_stack[q], 16)
                    sp.dma_start(ks[16 * r:16 * r + 16, q, :, :],
                                 k_scr[q, KPART[r]].rearrange("(h d) s -> d h s", d=HD)).then_inc(d_stack[q], 16)

            def weights(e):
                n, turn = RING[e]
                if turn >= 1:
                    sp.wait_ge(e_dn, (e - NPRE - NRING) // 2 + 1)
                t = ew[n]
                sp.dma_start(t[:, 0:EWG].rearrange("p (k f) -> p k f", k=HK),
                             wgu[e].rearrange("(k p) f -> p k f", p=P)).then_inc(d_ew[n], 16)
                sp.dma_start(t[:, EWG:EWG + H], wd[e, 0:P, :]).then_inc(d_ew[n], 16)
                sp.dma_start(t[0:I - P, EWG + H:EWG + EWD], wd[e, P:I, :]).then_inc(d_ew[n], 16)

            sp.wait_ge(s_const, 1)
            stack_out(0)
            stack_in(0)
            sp.dma_start(wo_s[:, :, :], wo).then_inc(d_c1, 16)
            sp.dma_start(gate_s[:, :, :], gate.rearrange("(k p) o -> p k o", p=P)).then_inc(d_c1, 16)
            sp.dma_start(keys[:, :, :], keys_in).then_inc(d_c1, 16)
            sp.dma_start(tri[:, :, :], tri_in).then_inc(d_c1, 16)
            sp.dma_start(emask[:, :, :], emask_in).then_inc(d_c1, 16)
            sp.dma_start(pad[:, :], pad_in).then_inc(d_c1, 16)
            sp.dma_start(wsgu_s[:, :, :], wsgu.rearrange("(k p) o -> p k o", p=P)).then_inc(d_wsh, 16)
            sp.dma_start(wsd_s[:, 0:2, :], wsd[0:2 * P, :].rearrange("(k p) o -> p k o", p=P)).then_inc(d_wsh, 16)
            sp.dma_start(wsd_s[0:ISH - 2 * P, 2, :], wsd[2 * P:ISH, :]).then_inc(d_wsh, 16)
            sp.dma_start(x_scr[T:ROWS, :], zero[:, :]).then_inc(d_scr, 16)
            for t in range(END + 1):
                for name, b in products_at(t - 1):
                    if name == "MT":
                        g, q = b % NKV, b // NKV % 2
                        sp.wait_ge(s_mrow, b + 1)
                        if b >= 8:
                            sp.wait_ge(s_p2, 16 * (b - 7))
                        for j in range(3):
                            sp.dma_start(qs[MROW + j:MROW + j + 1, q, REP * g:REP * g + REP, :]
                                         .rearrange("o h (i p) -> o (h i) p", p=P),
                                         mrow[0:16, b % 2, j, :]).then_inc(d_mrow[b % 2], 16)
                    if name == "ST":
                        sp.wait_ge(s_row, b + 1)
                        sp.dma_start(x_scr[S * b:S * b + S, :].rearrange("(i p) w -> p i w", p=P),
                                     xr[:, :, :]).then_inc(d_scr, 16)
                if t % 64 == 36 and t // 64 + 1 < NB:
                    stack_out(t // 64 + 1)
                if t % 64 == 42 and t // 64 + 1 < NB:
                    stack_in(t // 64 + 1)
                if t < 16 * NPRE and t % 16 == 8:
                    weights(t // 16)
                if t % 8 == 3 and t // 8 < 2 * ROWS // P:
                    n = t // 8
                    sp.dma_start(plane[P * n:P * n + P, :], zero[:, 0:H]).then_inc(d_zero, 16)
                if t == UNITS + AVLAG:
                    sp.wait_ge(s_pad, 1)
                    for e in range(NPRE, NPRE + NRING):
                        weights(e)
            sp.wait_ge(s_best, NB)
            for i in range(NT):
                sp.dma_start(merged[:, C * i:C * i + C], best[E * i:E * i + E, :]).then_inc(d_merge, 16)
            for e in range(NPRE + NRING, E):
                weights(e)
            sp.wait_ge(d_plane, 16 * PAIRS)
            for n in range(NB * 2 + 1):
                if n < NB * 2:
                    q = n % 2
                    if n >= 2:
                        sp.wait_ge(s_fin, n - 1)
                    for half in range(2):
                        sp.dma_start(fin[:, q, half, :, :],
                                     plane[ROWS * half + 2 * P * n:ROWS * half + 2 * P * n + 2 * P, :]
                                     .rearrange("(i p) h -> p i h", p=P)).then_inc(d_fin[q], 16)
                if n >= 1:
                    sp.wait_ge(s_fin, n)
                    sp.dma_start(out[2 * P * (n - 1):2 * P * n, :].rearrange("(i p) h -> p i h", p=P),
                                 xs[:, 2 * (n - 1):2 * n, :]).then_inc(d_out, 16)
            sp.wait_ge(d_out, 16 * NB * 2)

        @block.tensor
        def _(pe):
            def product(p):
                name, b = p
                q = b % 2
                if name in ("T0", "T1"):
                    k = int(name[1])
                    if p == ORDER[0]:
                        pe.wait_ge(d_c0, 16 * 3)
                    pe.wait_ge(s_xn, NORM_AT[0, b])
                    wait_bank(pe, p)
                    for i in range(NT):
                        mm = pe.transpose(bank(p)[:, P * i:P * i + P], xn[:, i, P * k:P * k + P], ident[:, :])
                elif name in ("Q0", "Q1", "KV"):
                    if name == "Q0":
                        if b == 0:
                            pe.wait_ge(d_wqkv, 32)
                        wait_taken(pe, ("T0", b))
                        wait_taken(pe, ("T1", b))
                    w = wkv_s[:, :, :] if name == "KV" else wq_s[:, :, P * int(name[1]):P * int(name[1]) + P]
                    wait_bank(pe, p)
                    for k in range(HK):
                        mm = pe.matmul(bank(p), w[:, k, :], xt[:, k, :], start=(k == 0), stop=(k == HK - 1))
                elif name == "VT":
                    pe.wait_ge(s_v, b + 1)
                    wait_bank(pe, p)
                    for i in range(NT):
                        mm = pe.transpose(bank(p)[:, 64 * i:64 * i + 64], vt[64:P, P * i:P * i + P],
                                          ident[64:P, 64:P])
                elif name == "MT":
                    pe.wait_ge(s_max, 16 * (b + 1))
                    wait_bank(pe, p)
                    mm = pe.transpose(bank(p)[0:16, 0:P], mx[:, b % 2, :], ident[:, :])
                elif name in ("W0", "W1"):
                    if name == "W0":
                        pe.wait_ge(s_norm, NKV * (b + 1))
                        if b == 0:
                            pe.wait_ge(d_c1, 16 * 6)
                    wait_bank(pe, p)
                    for n in range(2):
                        i = 2 * int(name[1]) + n
                        for g in range(NKV):
                            mm = pe.matmul(bank(p)[:, H * n:H * n + H], ot[:, g, P * i:P * i + P], wo_s[:, g, :],
                                           start=(g == 0), stop=(g == NKV - 1))
                elif name in ("U0", "U1"):
                    k = int(name[1])
                    pe.wait_ge(s_xn, NORM_AT[1, b])
                    wait_bank(pe, p)
                    for i in range(NT):
                        mm = pe.transpose(bank(p)[:, P * i:P * i + P], xr[:, i, P * k:P * k + P], ident[:, :])
                elif name == "GL":
                    wait_taken(pe, ("U0", b))
                    wait_taken(pe, ("U1", b))
                    wait_bank(pe, p)
                    for k in range(HK):
                        for i in range(NT):
                            mm = pe.matmul(bank(p)[E * i:E * i + E, 0:P], gate_s[:, k, :], xrt[:, k, P * i:P * i + P],
                                           start=(k == 0), stop=(k == HK - 1), skip_group_check=True)
                elif name == "GT":
                    wait_taken(pe, ("GL", b))
                    wait_bank(pe, p)
                    mm = pe.transpose(bank(p)[:, 0:P], lgt[:, :], ident[:, :])
                elif name == "ST":
                    pe.wait_ge(s_sel, b + 1)
                    wait_bank(pe, p)
                    mm = pe.transpose(bank(p)[:, 0:P], sel[:, :, :], ident[:, :])
                elif name[0] == "A":
                    c, up = int(name[1]) // 2, int(name[1]) % 2
                    m = min(P, ISH - P * c)
                    if p == ("A0", 0):
                        pe.wait_ge(d_wsh, 16 * 3)
                    wait_bank(pe, p)
                    for k in range(HK):
                        mm = pe.matmul(bank(p)[0:m, :], wsgu_s[:, k, ISH * up + P * c:ISH * up + P * c + m],
                                       xrt[:, k, :], start=(k == 0), stop=(k == HK - 1))
                else:
                    wait_taken(pe, ("A5", b))
                    wait_bank(pe, p)
                    for n in range(2):
                        i = 2 * int(name[1]) + n
                        for c in range(3):
                            mm = pe.matmul(bank(p)[:, H * n:H * n + H], hs[:, c, P * i:P * i + P], wsd_s[:, c, :],
                                           start=(c == 0), stop=(c == 2))
                mm.then_inc(full(p), 1)

            for name in PROLOGUE:
                product((name, 0))
            for t in range(END):
                if t < UNITS:
                    s, hl, i = t // 16, t // 4 % 4, t % 4
                    b, g = s // NKV, s % NKV
                    if s % NKV == 0 and t % 16 == 0:
                        pe.wait_ge(d_stack[b % 2], 16 * 12 * (b // 2 + 1))
                    if t >= 2:
                        pe.wait_ge(s_max, t - 1)
                    pe.matmul(score[t % 2][:, 0, :], qs[0:MROW, b % 2, REP * g + hl, P * i:P * i + P],
                              ks[0:MROW, b % 2, g, :], start=True, stop=True).then_inc(s_p1, 1)
                v = t - LAG
                if 0 <= v < UNITS:
                    s, kt, hl = v // 16, v // 4 % 4, v % 4
                    b, g = s // NKV, s % NKV
                    if v % 16 == 0:
                        pe.wait_ge(d_mrow[s % 2], 16 * 3 * (s // 2 + 1))
                    if v >= NS:
                        pe.wait_ge(s_exp, v - NS + 1)
                    pe.matmul(ps_s[:, v % NS, :], ks[0:KR, b % 2, g, P * kt:P * kt + P],
                              qs[0:KR, b % 2, REP * g + hl, :], start=True, stop=True).then_inc(s_p2, 1)
                if 0 <= t - AVLAG < UNITS and (t - AVLAG) % 4 == 0:
                    n = (t - AVLAG) // 4
                    s, kt = n // 4, n % 4
                    pe.wait_ge(s_exp, 4 * n + 4)
                    if kt == 0 and s >= 1:
                        pe.wait_ge(s_norm, s)
                    if kt == 0 and s % NKV == 0:
                        wait_taken(pe, ("VT", s // NKV))
                    for hl in range(REP):
                        mm = pe.matmul(ps_o[32 * hl:32 * hl + 32, 0, :], vs[:, s // NKV % 2, kt, s % NKV, :],
                                       pt[:, n % NP, hl, :], start=(kt == 0), stop=(kt == 3), skip_group_check=True)
                    mm.then_inc(s_av, 1)
                for p in products_at(t):
                    product(p)

            pe.wait_ge(s_tk, 1)
            n = len(ORDER)
            pe.wait_ge(m_taken[n % 2], n // 2)
            for half in range(2):
                mm = pe.matmul(ps_m[64 * half:64 * half + 64, n % 2, 0:PAIRS], best2[:, :],
                               ident[0:E, half:E:2], start=True, stop=True, skip_group_check=True)
            mm.then_inc(s_idp, 1)

            def x_turn(j):
                pe.wait_ge(d_gather, 16 * PAIRS)
                if j >= 2:
                    pe.wait_ge(e_xtc, j - 1)
                for k in range(HK):
                    mm = pe.transpose(score[j % 2][:, 0, P * k:P * k + P], xg[:, j, P * k:P * k + P], ident[:, :])
                mm.then_inc(e_xt, 1)

            def gate_up(j):
                pe.wait_ge(e_xtc, j + 1)
                if j >= 2:
                    pe.wait_ge(e_act, j - 1)
                for half in range(2):
                    slot, turn = RING[2 * j + half]
                    pe.wait_ge(d_ew[slot], 48 * (turn + 1))
                for k in range(HK):
                    for half in range(2):
                        w = ew[RING[2 * j + half][0]]
                        mm = pe.matmul(ps_s[64 * half:64 * half + 64, j % 2, 0:2 * I],
                                       xgt[:, j % 2, k, 64 * half:64 * half + 64],
                                       w[:, 2 * I * k:2 * I * k + 2 * I],
                                       start=(k == 0), stop=(k == HK - 1), skip_group_check=True)
                mm.then_inc(e_gu, 1)

            def act_turn(j):
                pe.wait_ge(e_act, j + 1)
                if j >= 1:
                    pe.wait_ge(e_atc, j)
                pe.transpose(ps_o[:, 0, 0:P], egu[:, 2 + j % 2, 0:P], ident[:, :])
                pe.transpose(ps_o[0:I - P, 0, P:2 * P], egu[:, 2 + j % 2, P:I], ident[:, :]).then_inc(e_at, 1)

            def down(j):
                pe.wait_ge(e_atc, j + 1)
                if j >= 2:
                    pe.wait_ge(e_y, j - 1)
                for k in range(2):
                    for half in range(2):
                        w = ew[RING[2 * j + half][0]]
                        mm = pe.matmul(ps_m[64 * half:64 * half + 64, j % 2, 0:H],
                                       eat[:, j % 2, k, 64 * half:64 * half + 64],
                                       w[:, EWG + H * k:EWG + H * k + H],
                                       start=(k == 0), stop=(k == 1), skip_group_check=True)
                mm.then_inc(e_dn, 1)

            pe.wait_ge(s_idx, 1)
            for j in range(-2, PAIRS):
                if j + 2 < PAIRS:
                    x_turn(j + 2)
                if 0 <= j + 1 < PAIRS:
                    gate_up(j + 1)
                if j >= 0:
                    act_turn(j)
                    down(j)

        @block.scalar
        def _(act):
            def consume(p):
                name, b = p
                if name in ("T0", "T1", "U0", "U1"):
                    dst = (xt if name[0] == "T" else xrt)[:, int(name[1]), :]
                    wait_product(act, p)
                    if name == "T0" and b > 0:
                        wait_product(act, ("KV", b - 1))
                    if name == "U0" and b > 0:
                        wait_product(act, ("A5", b - 1))
                    nc.scalar.activation(dst, bank(p), ACT.Copy).then_inc(taken(p), 1)
                if name == "VT":
                    wait_product(act, p)
                    if b >= 2:
                        act.wait_ge(s_av, 16 * (b - 1))
                    nc.scalar.activation(vs[:, b % 2, :, :, 0:HD],
                                         bank(p)[:, 0:NT * NKV * HD].rearrange("p (i g d) -> p i g d", i=NT, g=NKV),
                                         ACT.Copy).then_inc(taken(p), 1)
                if name == "GL":
                    wait_product(act, p)
                    nc.scalar.activation(lgt[:, :], bank(p)[:, 0:P], ACT.Copy).then_inc(taken(p), 1)
                if name in ("A1", "A3", "A5"):
                    c = int(name[1]) // 2
                    g = (f"A{2 * c}", b)
                    m = min(P, ISH - P * c)
                    wait_product(act, g)
                    if (c, b) != (0, 0):
                        wait_taken(act, (f"A{2 * c - 1}", b) if c else ("A5", b - 1))
                    nc.scalar.activation(th[0:m, :], bank(g)[0:m, :], ACT.Tanh, scale=0.5).then_inc(s_tanh, 1)

            def gate_exp(b):
                act.wait_ge(s_mask, b + 1)
                nc.scalar.activation(ex[:, :, :], lg[:, :, :], ACT.Exp).then_inc(s_ex, 1)

            for name in PROLOGUE:
                consume((name, 0))
            for t in range(END + 1):
                v = t - LAG
                if 0 <= v < UNITS:
                    n, hl = v // 4, v % 4
                    act.wait_ge(s_p2, v + 1)
                    if n >= NP and hl == 0:
                        act.wait_ge(s_av, n - NP + 1)
                    nc.scalar.activation(pt[:, n % NP, hl, :], ps_s[:, v % NS, :], ACT.Exp,
                                         scale=ATT_SCALE).then_inc(s_exp, 1)
                for p in products_at(t - 1):
                    consume(p)
                for p in products_at(t - 7):
                    if p[0] == "GT":
                        gate_exp(p[1])
            for j in range(-2, PAIRS):
                if j + 2 < PAIRS:
                    n = j + 2
                    act.wait_ge(e_xt, n + 1)
                    if n >= 2:
                        act.wait_ge(e_gu, n - 1)
                    nc.scalar.activation(xgt[:, n % 2, :, :], score[n % 2][:, 0, 0:H].rearrange("p (k c) -> p k c", k=HK),
                                         ACT.Copy).then_inc(e_xtc, 1)
                if 0 <= j + 1 < PAIRS:
                    n = j + 1
                    act.wait_ge(e_gu, n + 1)
                    if n >= 2:
                        act.wait_ge(e_act, n - 1)
                    nc.scalar.activation(egu[:, n % 2, :], ps_s[:, n % 2, 0:I], ACT.Tanh, scale=0.5).then_inc(e_th, 1)
                if j >= 0:
                    act.wait_ge(e_dn, j + 1)
                    if j == 0:
                        act.wait_ge(s_ws, PAIRS)
                    if j >= 2:
                        act.wait_ge(d_plane, 16 * (j - 1))
                    nc.scalar.activation(ey[:, j % 2, :], ps_m[:, j % 2, 0:H], ACT.Copy,
                                         scale=wslot[:, j:j + 1]).then_inc(e_y, 1)

        @block.gpsimd
        def _(pool):
            count = [0]

            def link(ins):
                count[0] += 1
                ins.then_inc(s_pool, 1)
                pool.wait_ge(s_pool, count[0])

            def rope(p):
                name, b = p
                c = ("Q0", "Q1", "KV").index(name)
                n = 3 * b + c
                m = P if c < 2 else NKV * HD
                wait_product(pool, p)
                wait_taken(pool, p)
                link(nc.gpsimd.tensor_tensor(qb[0:m, c, :], qb[0:m, c, :], sin_s[0:m, :], ALU.mult))
                nc.gpsimd.tensor_tensor(qa[0:m, c, :], qa[0:m, c, :], qb[0:m, c, :], ALU.add).then_inc(s_roped, 1)
                pool.wait_ge(s_roped, n + 1)
                pool.wait_ge(s_hi, n + 1)
                nc.gpsimd.tensor_tensor(qa[0:m, c, :], qa[0:m, c, :], part[0:m, 0, c, :], ALU.subtract).then_inc(s_res, 1)
                pool.wait_ge(s_res, n + 1)
                pool.wait_ge(s_mid, n + 1)
                nc.gpsimd.tensor_tensor(part[0:m, 2, c, :], qa[0:m, c, :], part[0:m, 1, c, :], ALU.subtract).then_inc(s_lo, 1)

            def root(n, which):
                pool.wait_ge(s_var, n)
                nc.gpsimd.tensor_tensor(rstd[:, which, :], rstd[:, which, :], halfs[:, :], ALU.pow).then_inc(s_rstd, 1)

            root(1, 0)
            for name in ("Q0", "Q1", "KV"):
                rope((name, 0))
            for t in range(END + 1):
                for kind, bb in norms_at(t):
                    root(NORM_AT[kind, bb], kind)
                for p in products_at(t - 1):
                    if p[0] in ("Q0", "Q1", "KV"):
                        rope(p)
            pool.wait_ge(s_idx, 2)
            pool.wait_ge(d_scr, 16 * (NB + 1))
            pool.wait_ge(s_exp, UNITS)
            pool.wait_ge(s_av, UNITS // 4)
            for j in range(PAIRS):
                nc.gpsimd.indirect_dma_start(out=xg[:, j, :], out_offset=None, in_=x_scr,
                                             in_offset=bass.IndirectOffsetOnAxis(ap=idx[:, 0, j:j + 1], axis=0),
                                             ).then_inc(d_gather, 16)
            pool.wait_ge(d_zero, 16 * (2 * ROWS // P))
            for j in range(PAIRS):
                pool.wait_ge(e_y, j + 1)
                if j >= 1:
                    pool.wait_ge(d_plane, 16 * j)
                nc.gpsimd.indirect_dma_start(out=plane, in_=ey[:, j % 2, :], in_offset=None,
                                             out_offset=bass.IndirectOffsetOnAxis(ap=idx[:, 1, j:j + 1], axis=0),
                                             compute_op=ALU.add).then_inc(d_plane, 16)
            pool.wait_ge(d_plane, 16 * PAIRS)

        @block.vector
        def _(dve):
            count = [0]

            def link(ins):
                count[0] += 1
                ins.then_inc(s_dve, 1)
                dve.wait_ge(s_dve, count[0])

            V = nc.vector
            for tile in (zero, cand, best2):
                V.memset(tile[:], 0.0)
            V.memset(wsd_s[ISH - 2 * P:P, 2, :], 0.0)
            V.memset(hs[ISH - 2 * P:P, 2, :], 0.0)
            for n in range(NPRE):
                V.memset(ew[n][:, EWG + H:EWG + EWD], 0.0)
            V.memset(halfs[:], -0.5)
            V.memset(ks[MROW:P, :, :, :], 1.0)
            V.memset(vs[:, :, :, :, HD:2 * HD], 1.0).then_inc(s_const, 1)
            dve.wait_ge(s_const, 1)

            def norm_stats(src, which):
                for i in range(NT):
                    ins = V.bn_stats(stat[:, which, i, :], src(i))
                link(ins)
                for i in range(NT):
                    ins = V.bn_aggr(agg[:, which, i, :], stat[:, which, i, :])
                link(ins)
                V.tensor_scalar(rstd[:, which, :], agg[:, which, :, 1], EPS, None, ALU.add).then_inc(s_var, 1)

            def norm_apply(src, dst, which, n):
                dve.wait_ge(s_rstd, n)
                for i in range(NT):
                    ins = V.tensor_scalar(dst(i), src(i), agg[:, which, i, 0:1], rstd[:, which, i:i + 1],
                                          ALU.subtract, ALU.mult)
                ins.then_inc(s_xn, 1)

            def stats(kind, b):
                if kind == 0:
                    dve.wait_ge(d_x[b], 16)
                norm_stats(lambda i: xs[:, NT * b + i, :], kind)

            def apply(kind, b):
                if kind == 0:
                    if b > 0:
                        wait_product(dve, ("T1", b - 1))
                        wait_product(dve, ("T0", b - 1))
                    norm_apply(lambda i: xs[:, NT * b + i, :], lambda i: xn[:, i, :], 0, NORM_AT[0, b])
                else:
                    if b > 0:
                        dve.wait_ge(d_scr, 16 * (b + 1))
                    norm_apply(lambda i: xs[:, NT * b + i, :], lambda i: xr[:, i, 0:H], 1, NORM_AT[1, b])

            def route(b, p):
                wait_product(dve, p)
                V.tensor_copy(lg[:, :, :], bank(p)[:, 0:P].rearrange("p (i e) -> p i e", i=NT)).then_inc(taken(p), 1)
                wait_taken(dve, p)
                link(V.tensor_reduce(gs[:, :, :], lg[:, :, :].rearrange("p i (g e) -> p (i g) e", g=G), AX.X, ALU.max))
                for i in range(NT):
                    mine = gs[:, i, :, None].broadcast_to([P, G, G])
                    other = gs[:, i, None, :].broadcast_to([P, G, G])
                    V.tensor_tensor(cmp[:, i, :, :], other, mine, ALU.is_gt)
                    ins = V.tensor_tensor(eq[:, i, :, :], other, mine, ALU.is_equal)
                link(ins)
                for i in range(NT):
                    ins = V.tensor_tensor(eq[:, i, :, :], eq[:, i, :, :], tri[:, :, :], ALU.mult)
                link(ins)
                link(V.tensor_tensor(cmp[:, :, :, :], cmp[:, :, :, :], eq[:, :, :, :], ALU.add))
                link(V.tensor_reduce(rank[:, :, :], cmp[:, :, :, :].rearrange("p i a c -> p (i a) c"), AX.X, ALU.add))
                link(V.tensor_scalar(rank[:, :, :], rank[:, :, :], TG - 0.5, None, ALU.is_lt))
                keep = rank[:, :, :].rearrange("p i g -> p (i g)")[:, :, None].broadcast_to([P, NT * G, EG])
                lgv = lg[:, :, :].rearrange("p i (g e) -> p (i g) e", g=G)
                link(V.tensor_tensor(lgv, lgv, keep, ALU.mult))
                link(V.tensor_reduce(exs[:, :, 0], lg[:, :, :], AX.X, ALU.max))
                V.tensor_tensor(lg[:, :, :], lg[:, :, :], exs[:, :, 0:1].broadcast_to([P, NT, E]),
                                ALU.subtract).then_inc(s_mask, 1)

            def choose(b):
                dve.wait_ge(s_ex, b + 1)
                V.tensor_reduce(exs[:, :, 1], ex[:, :, :], AX.X, ALU.add)
                for i in range(NT):
                    ins = V.max(top[:, i, :], ex[:, i, :])
                link(ins)
                V.reciprocal(exs[:, :, 2:3], exs[:, :, 1:2])
                link(V.memset(top[:, :, TOPK:8], -5.0))
                for i in range(NT):
                    ins = V.match_replace(out=rep[:, i, :], in_to_replace=top[:, i, :], in_values=ex[:, i, :],
                                          imm_value=-1.0)
                link(ins)
                link(V.tensor_scalar(exs[:, :, 3:4], exs[:, :, 2:3], SCALE_W, None, ALU.mult))
                V.tensor_scalar(sel[:, :, :], rep[:, :, :], 0.0, None, ALU.is_lt).then_inc(s_sel, 1)
                V.tensor_tensor(xr[:, :, H:XW], ex[:, :, :], exs[:, :, 3:4].broadcast_to([P, NT, E]),
                                ALU.mult).then_inc(s_row, 1)

            def best_keys(src, dst, n, done):
                for r in range(n // 8):
                    if r:
                        link(V.match_replace(out=src, in_to_replace=dst[:, 8 * r - 8:8 * r], in_values=src,
                                             imm_value=0.0))
                    ins = V.max(dst[:, 8 * r:8 * r + 8], src)
                    if r == n // 8 - 1:
                        done(ins)
                    else:
                        link(ins)

            def consume(p):
                name, b = p
                if name in ("Q0", "Q1", "KV"):
                    c = ("Q0", "Q1", "KV").index(name)
                    n = 3 * b + c
                    m = P if c < 2 else NKV * HD
                    wait_product(dve, p)
                    if p == ("Q0", 0):
                        dve.wait_ge(d_c0, 48)
                    if b > 0:
                        dve.wait_ge(s_lo, n - 2)
                    if c == 2:
                        if b > 0:
                            wait_product(dve, ("VT", b - 1))
                        V.tensor_copy(vt[64:P, :], bank(p)[64:P, :]).then_inc(s_v, 1)
                    V.stream_shuffle(qb[0:m, c, :], bank(p)[0:m, :], [i ^ 8 for i in range(32)])
                    V.tensor_tensor(qa[0:m, c, :], bank(p)[0:m, :], cos_s[0:m, :], ALU.mult).then_inc(taken(p), 1)
                if name == "MT":
                    wait_product(dve, p)
                    if b >= 2:
                        dve.wait_ge(d_mrow[b % 2], 48 * (b // 2))
                    row = mrow[:, b % 2, :, :]
                    link(V.tensor_scalar(row[:, 0, :], bank(p)[0:16, 0:P], -1.0, None, ALU.mult))
                    link(V.scalar_tensor_tensor(out=mr[:, :], in0=bank(p)[0:16, 0:P], scalar=-1.0, in1=row[:, 0, :],
                                                op0=ALU.mult, op1=ALU.subtract))
                    V.tensor_copy(row[:, 1, :], mr[:, :]).then_inc(taken(p), 1)
                    wait_taken(dve, p)
                    V.tensor_tensor(row[:, 2, :], mr[:, :], row[:, 1, :], ALU.subtract).then_inc(s_mrow, 1)
                if name in ("W0", "W1", "D0", "D1"):
                    i = NT * b + 2 * int(name[1])
                    wait_product(dve, p)
                    V.tensor_tensor(xs[:, i:i + 2, :], xs[:, i:i + 2, :],
                                    bank(p).rearrange("p (n h) -> p n h", n=2), ALU.add).then_inc(taken(p), 1)
                    wait_taken(dve, p)
                if name == "GT":
                    route(b, p)
                if name in ("A1", "A3", "A5"):
                    c = int(name[1]) // 2
                    g = (f"A{2 * c}", b)
                    m = min(P, ISH - P * c)
                    dve.wait_ge(s_tanh, 3 * b + c + 1)
                    wait_product(dve, p)
                    if c == 0 and b > 0:
                        wait_product(dve, ("D1", b - 1))
                    V.scalar_tensor_tensor(out=hs[0:m, c, :], in0=th[0:m, :], scalar=1.0, in1=bank(g)[0:m, :],
                                           op0=ALU.add, op1=ALU.mult).then_inc(taken(g), 1)
                    wait_taken(dve, g)
                    V.scalar_tensor_tensor(out=hs[0:m, c, :], in0=hs[0:m, c, :], scalar=0.5, in1=bank(p)[0:m, :],
                                           op0=ALU.mult, op1=ALU.mult).then_inc(taken(p), 1)
                if name == "ST":
                    wait_product(dve, p)
                    if b == 0:
                        dve.wait_ge(d_c1, 16 * 6)
                    V.tensor_tensor(cand[:, C:C + P], bank(p)[:, 0:P], keys[:, b, :], ALU.mult).then_inc(taken(p), 1)
                    wait_taken(dve, p)
                    if b > 0:
                        dve.wait_ge(s_best, b)
                    best_keys(cand[:, :], best, C, link)
                    V.tensor_copy(cand[:, 0:C], best[:, :]).then_inc(s_best, 1)

            stats(0, 0)
            apply(0, 0)
            def high(p):
                c = ("Q0", "Q1", "KV").index(p[0])
                n, m = 3 * p[1] + c, P if c < 2 else NKV * HD
                dve.wait_ge(s_roped, n + 1)
                if p[1] > 0:
                    dve.wait_ge(d_part[(p[1] - 1) % 2], 16 * 9 * ((p[1] - 1) // 2 + 1))
                V.tensor_copy(part[0:m, 0, c, :], qa[0:m, c, :]).then_inc(s_hi, 1)

            def middle(p):
                c = ("Q0", "Q1", "KV").index(p[0])
                n, m = 3 * p[1] + c, P if c < 2 else NKV * HD
                dve.wait_ge(s_res, n + 1)
                V.tensor_copy(part[0:m, 1, c, :], qa[0:m, c, :]).then_inc(s_mid, 1)

            for name in PROLOGUE:
                consume((name, 0))
            for name in ("Q0", "Q1", "KV"):
                high((name, 0))
                middle((name, 0))
            for t in range(END + 1):
                if t < UNITS:
                    s, u = t // 16, t % 16
                    dve.wait_ge(s_p1, t + 1)
                    if u == 0 and s >= 2:
                        wait_product(dve, ("MT", s - 2))
                    V.tensor_reduce(mx[:, s % 2, u:u + 1], score[t % 2][:, 0, :], AX.X, ALU.max).then_inc(s_max, 1)
                for kind, bb in norms_at(t):
                    stats(kind, bb)
                for kind, bb in norms_at(t - 2):
                    apply(kind, bb)
                for p in products_at(t - 1):
                    consume(p)
                for p in products_at(t - 4):
                    if p[0] in ("Q0", "Q1", "KV"):
                        high(p)
                for p in products_at(t - 7):
                    if p[0] in ("Q0", "Q1", "KV"):
                        middle(p)
                for p in products_at(t - 9):
                    if p[0] == "GT":
                        choose(p[1])
                if (t - AVLAG - 13) % 16 == 0 and 0 <= (t - AVLAG - 13) // 16 < STEPS:
                    s = (t - AVLAG - 13) // 16
                    b, g = s // NKV, s % NKV
                    dve.wait_ge(s_av, 4 * s + 4)
                    if g == 0 and b > 0:
                        wait_product(dve, ("W1", b - 1))
                    link(V.reciprocal(rec[:, :], ps_o[:, 0, :]))
                    link(V.stream_shuffle(recs[:, :], rec[:, :], [16 + i % 16 for i in range(32)]))
                    V.tensor_tensor(ot[:, g, :], ps_o[:, 0, :], recs[:, :], ALU.mult).then_inc(s_norm, 1)
            dve.wait_ge(s_av, UNITS // 4)
            for n in range(NPRE, NPRE + NRING):
                V.memset(ew[n][:, EWG + H:EWG + EWD], 0.0)
            V.memset(eat[:, :, 1, :], 0.0).then_inc(s_pad, 1)
            dve.wait_ge(d_merge, 16 * NT)
            best_keys(merged[:, :], best2, C, lambda ins: ins.then_inc(s_tk, 1))
            dve.wait_ge(s_idp, 1)
            keyp = ps_m[:, len(ORDER) % 2, 0:PAIRS]
            V.tensor_scalar(idz[:, :], keyp, 0.0, pad[:, 0:1], ALU.is_equal, ALU.mult)
            link(V.tensor_scalar(idf[:, :], keyp, -1.0, float(T), ALU.mult, ALU.add))
            link(V.tensor_tensor(idf[:, :], idf[:, :], idz[:, :], ALU.add))
            V.tensor_copy(idx[:, 0, :], idf[:, :]).then_inc(s_idx, 1)
            V.tensor_scalar(idx[:, 1, :], idf[:, :], pad[:, 1:2], None, ALU.add).then_inc(s_idx, 1)
            dve.wait_ge(d_gather, 16 * PAIRS)
            for j in range(PAIRS):
                V.tensor_tensor_reduce(out=wtmp[:, j, :], in0=xg[:, j, H:XW], in1=emask[:, j, :], scale=1.0,
                                       scalar=0.0, op0=ALU.mult, op1=ALU.add,
                                       accum_out=wslot[:, j:j + 1]).then_inc(s_ws, 1)
            for j in range(-1, PAIRS):
                n = j + 1
                if n < PAIRS:
                    dve.wait_ge(e_th, n + 1)
                    if n >= 2:
                        dve.wait_ge(e_at, n - 1)
                    a = egu[:, 2 + n % 2, :]
                    link(V.scalar_tensor_tensor(out=a, in0=egu[:, n % 2, :], scalar=1.0, in1=ps_s[:, n % 2, 0:I],
                                                op0=ALU.add, op1=ALU.mult))
                    V.scalar_tensor_tensor(out=a, in0=a, scalar=0.5, in1=ps_s[:, n % 2, I:2 * I],
                                           op0=ALU.mult, op1=ALU.mult).then_inc(e_act, 1)
                if j >= 0:
                    dve.wait_ge(e_at, j + 1)
                    if j >= 2:
                        dve.wait_ge(e_dn, j - 1)
                    V.tensor_copy(eat[:, j % 2, 0, :], ps_o[:, 0, 0:P])
                    V.tensor_copy(eat[0:I - P, j % 2, 1, :], ps_o[0:I - P, 0, P:2 * P]).then_inc(e_atc, 1)
            for n in range(NB * 2):
                q = n % 2
                dve.wait_ge(d_fin[q], 32 * (n // 2 + 1))
                link(V.tensor_tensor(xs[:, 2 * n:2 * n + 2, :], xs[:, 2 * n:2 * n + 2, :], fin[:, q, 0, :, :], ALU.add))
                V.tensor_tensor(xs[:, 2 * n:2 * n + 2, :], xs[:, 2 * n:2 * n + 2, :], fin[:, q, 1, :, :],
                                ALU.add).then_inc(s_fin, 1)


def kernel(**inputs):
    import numpy as np
    import concourse.bacc as bacc
    from concourse.bass_utils import run_bass_kernel_spmd as run

    f = np.float32
    a = {k[3:]: np.ascontiguousarray(v) for k, v in inputs.items()}
    wo = np.zeros((REP, 2 * HD, NKV, H), f)
    wo[:, :HD] = a["attn_Wo"].T.reshape(NKV, REP, HD, H).transpose(1, 2, 0, 3)
    inv = (f(1.0) / f(10000.0) ** (np.arange(0, HD, 2, dtype=f) / f(HD))).astype(f)
    ang = np.arange(S, dtype=f)[None, :] * np.concatenate([inv, inv])[:, None]
    sign = np.where(np.arange(HD) < HD // 2, -1, 1).astype(f)[:, None]
    p, j = np.arange(P), np.arange(PAIRS)
    tile, lane = np.arange(P)[:, None, None] // E, np.arange(P)[None, None, :]
    token = S * np.arange(NB)[None, :, None] + P * tile + lane
    arrays = {
        "x": a["attn_x"].reshape(T, H),
        "wq": np.ascontiguousarray(a["attn_Wq"].T),
        "wkv": np.ascontiguousarray(np.concatenate([a["attn_Wk"], a["attn_Wv"]]).T),
        "wo": wo.reshape(P, NKV, H),
        "gate": np.ascontiguousarray(a["ffn_gate_w"].T),
        "wsgu": a["ffn_ws_gate_up"], "wsd": a["ffn_ws_down"],
        "wgu": a["ffn_w_gate_up"], "wd": a["ffn_w_down"],
        "cosr": np.tile(np.cos(ang), (P // HD, 1)).astype(f),
        "sinr": np.tile(np.sin(ang) * sign, (P // HD, 1)).astype(f),
        "ident_in": np.eye(P, dtype=f),
        "keys_in": (T - token).astype(f),
        "tri_in": np.ascontiguousarray(np.broadcast_to(np.tri(G, k=-1, dtype=f), (P, G, G))),
        "emask_in": (np.arange(E)[None, None, :] == (2 * j[None, :] + (p >= 64)[:, None])[:, :, None]).astype(f),
        "pad_in": np.stack([p, ROWS * (p >= 64)], 1).astype(f),
    }
    nc = bacc.Bacc("TRN2", target_bir_lowering=False, num_devices=1)
    args = [nc.dram_tensor(f"in_{k}", v.shape, mybir.dt.from_np(v.dtype), kind="ExternalInput").ap()
            for k, v in arrays.items()]
    out = nc.dram_tensor("out_0", (T, H), F32, kind="ExternalOutput").ap()
    moe_kernel(nc, *args, out)
    r = run(nc, [{f"in_{k}": v for k, v in arrays.items()}], core_ids=[0])
    return r.results[0]["out_0"].reshape(NB, S, H)
```

```python
from contextlib import ExitStack

import concourse.bass as bass
from concourse import mybir

F32 = mybir.dt.float32
BF16 = mybir.dt.bfloat16
U32 = mybir.dt.uint32
ALU = mybir.AluOpType
ACT = mybir.ActivationFunctionType
AX = mybir.AxisListType

P = 128
NB, S, H = 4, 512, 256
T = NB * S
NT = S // P
HK = H // P
NH, NKV = 16, 4
HD = H // NH
REP = NH // NKV
E, I, TOPK, C = 32, 176, 6, 48
G, TG = 8, 3
EG = E // G
ISH = 2 * I
SCALE_W = 16.0
EPS = 1e-5
ATT_SCALE = float(HD) ** -0.5
PAIRS = E // 2
ROWS = T + P
XW = H + E
MROW = 96
KR = 99
QPART = (0, 0, 1, 1, 0, 2)
KPART = (0, 1, 0, 1, 2, 0)

STEPS = NB * NKV
UNITS = STEPS * 16
LAG = 22
AVLAG = LAG + 6
NP, NS = 3, 3
END = UNITS + 84

PRE = [(8, "T0", 1), (9, "T1", 1), (11, "Q0", 2), (17, "Q1", 2), (23, "KV", 2), (27, "VT", 1)]
POST = [(28, "OT0", 1), (29, "OT1", 1), (30, "W0", 2), (33, "W1", 2), (39, "U0", 1), (40, "U1", 1),
        (43, "GL", 1), (46, "GT", 1), (49, "A0", 2), (51, "A1", 2), (53, "A2", 2), (55, "A3", 2),
        (59, "A4", 2), (61, "A5", 2), (63, "ST", 1), (65, "D0", 3), (69, "D1", 3)]
LAST = [p for p in POST if p[0] < 49] + [
    (48, "A0", 2), (50, "A1", 2), (56, "ST", 1), (58, "A2", 2), (60, "A3", 2), (63, "KP", 1),
    (65, "A4", 2), (67, "A5", 2), (70, "D0", 3), (74, "D1", 3)]
PROLOGUE = ["T0", "T1", "Q0", "Q1", "KV", "VT"]
STACK_OUT, STACK_IN = 36, 43
FREE_EARLY = 64 * (NB - 2) + 48
FREE_ALL = UNITS + AVLAG + 2
NORM1, NORM2 = 4, 36


def table():
    out = [(16 * (s + 1), "MT", s, 1) for s in range(STEPS)]
    out += [(16 * s + AVLAG + 14, "NT", s, 1) for s in range(STEPS)]
    out += [(64 * (b - 1) + u, n, b, w) for b in range(1, NB) for u, n, w in PRE]
    out += [(64 * (b + 1) + u, n, b, w) for b in range(NB - 1) for u, n, w in POST]
    out += [(64 * NB + u, n, NB - 1, w) for u, n, w in LAST]
    return sorted(out)


TABLE = table()
for (t0, n0, _, w0), (t1, n1, _, _) in zip(TABLE, TABLE[1:]):
    assert t0 + w0 <= t1, (t0, n0, w0, t1, n1)
ORDER = [(n, 0) for n in PROLOGUE] + [(n, b) for _, n, b, _ in TABLE]
PLACE = {p: n for n, p in enumerate(ORDER)}


def parts_at(t):
    return [((n, b), t - u, w) for u, n, b, w in TABLE if u <= t < u + w]


def products_at(t):
    return [(n, b) for u, n, b, w in TABLE if u + w - 1 == t]


def norms_at(t):
    out = [(0, t // 64 + 1)] if t % 64 == NORM1 and 0 <= t and t // 64 + 1 < NB else []
    return out + ([(1, t // 64 - 1)] if t % 64 == NORM2 and t >= 64 and t // 64 - 1 < NB else [])


NORMS = [(0, 0)] + [n for t in range(END) for n in norms_at(t)]
NORM_AT = {n: i + 1 for i, n in enumerate(NORMS)}


def moe_kernel(nc, x, wq, wkv, wo, gate, wsgu, wsd, wgu, wd, cosr, sinr, ident_in, keys_in, tri_in,
               emask_in, pad_in, out):
    x_scr = nc.dram_tensor("x_scr", [ROWS, XW], F32).ap()
    plane = nc.dram_tensor("plane", [2 * ROWS, H], F32).ap()
    q_scr = nc.dram_tensor("q_scr", [2, 3, H, S], BF16).ap()
    k_scr = nc.dram_tensor("k_scr", [2, 3, NKV * HD, S], BF16).ap()

    with ExitStack() as ctx:
        def sb(name, shape, dt=F32):
            return ctx.enter_context(nc.sbuf_tensor(name, shape, dt))

        def sem(name):
            return ctx.enter_context(nc.semaphore(name))

        ps_a = ctx.enter_context(nc.psum_tensor("ps_a", [P, 1, S], F32))
        ps_a2 = ctx.enter_context(nc.psum_tensor("ps_a2", [P, 1, S], F32))
        ps_s = ctx.enter_context(nc.psum_tensor("ps_s", [P, NS, S], F32))
        ps_o = ctx.enter_context(nc.psum_tensor("ps_o", [P, 1, S], F32))
        ps_m = ctx.enter_context(nc.psum_tensor("ps_m", [P, 2, S], F32))
        score = [ps_a, ps_a2]

        xs = sb("xs", [P, NB * NT, H])
        wq_s, wkv_s = sb("wq_s", [P, HK, H]), sb("wkv_s", [P, HK, P])
        wo_s, gate_s = sb("wo_s", [P, HK, H]), sb("gate_s", [P, HK, E])
        wsgu_s, wsd_s = sb("wsgu_s", [P, HK, 2 * ISH]), sb("wsd_s", [P, 3, H])
        cos_s, sin_s = sb("cos_s", [P, S]), sb("sin_s", [P, S])
        ident, keys = sb("ident", [P, P]), sb("keys", [P, NB, P])
        tri, emask, pad = sb("tri", [P, G, G]), sb("emask", [P, PAIRS, E]), sb("pad", [P, 2])
        early = sb("early", [P, 2 * NT * H + 6 * S + 9 * S // 2])
        xn = early[:, 0:NT * H].rearrange("p (i h) -> p i h", i=NT)
        xt = early[:, NT * H:2 * NT * H].rearrange("p (k s) -> p k s", k=HK)
        qa = early[:, 2 * NT * H:2 * NT * H + 3 * S].rearrange("p (c s) -> p c s", c=3)
        qb = early[:, 2 * NT * H + 3 * S:2 * NT * H + 6 * S].rearrange("p (c s) -> p c s", c=3)
        part = early[:, 2 * NT * H + 6 * S:].bitcast(BF16).rearrange("p (j c s) -> p j c s", j=3, c=3)
        late = sb("late", [P, NT * XW + HK * S + 4 * S])
        xr = late[:, 0:NT * XW].rearrange("p (i w) -> p i w", i=NT)
        xrt = late[:, NT * XW:NT * XW + HK * S].rearrange("p (k s) -> p k s", k=HK)
        hs = late[:, NT * XW + HK * S:NT * XW + HK * S + 3 * S].rearrange("p (c s) -> p c s", c=3)
        th = late[:, NT * XW + HK * S + 3 * S:]
        fin = late[:, 0:16 * H].rearrange("p (n a i o) -> p n a i o", n=4, a=2, i=2)
        vt, vs = sb("vt", [P, S]), sb("vs", [P, 2, NT, NKV, 2 * HD])
        osb, rec = sb("osb", [P, S]), sb("rec", [P, NT, REP])
        od, ot = sb("od", [P, NT, H]), sb("ot", [P, HK, S])
        mx, mr, mrow = sb("mx", [P, 2, 16]), sb("mr", [16, P]), sb("mrow", [16, 2, 3, P], BF16)
        stat, agg = sb("stat", [P, 2, NT, 6]), sb("agg", [P, 2, NT, 2])
        rstd, halfs = sb("rstd", [P, 2, NT]), sb("halfs", [P, NT])
        lgt, lg = sb("lgt", [P, P]), sb("lg", [P, NT, E])
        gs, cmp, eq = sb("gs", [P, NT, G]), sb("cmp", [P, NT, G, G]), sb("eq", [P, NT, G, G])
        rank, ex, exs = sb("rank", [P, NT, G]), sb("ex", [P, NT, E]), sb("exs", [P, NT, 4])
        top, rep, sel = sb("top", [P, NT, 8]), sb("rep", [P, NT, E]), sb("sel", [P, NT, E])
        cand, best = sb("cand", [P, C + P]), sb("best", [P, C])
        merged, best2 = sb("merged", [E, 4 * C]), sb("best2", [E, 64])
        idf, idz, idx = sb("idf", [P, 16]), sb("idz", [P, 16]), sb("idx", [P, 2, 16], U32)
        wslot, wtmp = sb("wslot", [P, PAIRS]), sb("wtmp", [P, PAIRS, E])
        zero = sb("zero", [P, XW])

        QSB, KSB, PTB = 2 * NH * S // 2, 2 * NKV * S // 2, NP * REP * S
        big = sb("big", [P, QSB + KSB + PTB])
        qs = big[:, 0:QSB].bitcast(BF16).rearrange("p (b h s) -> p b h s", b=2, h=NH)
        ks = big[:, QSB:QSB + KSB].bitcast(BF16).rearrange("p (b h s) -> p b h s", b=2, h=NKV)
        pt = big[:, QSB + KSB:].rearrange("p (n h s) -> p n h s", n=NP, h=REP)
        EWG, EWD = HK * 2 * I, 2 * H
        NOWN = 6
        NEARLY = 5
        NRING = 6
        ew = [sb(f"ew{n}", [P, EWG + EWD]) for n in range(NOWN)]
        ew += [early[:, n * (EWG + EWD):(n + 1) * (EWG + EWD)] for n in range(NEARLY)]
        ew += [big[:, n * (EWG + EWD):(n + 1) * (EWG + EWD)] for n in range(NRING)]
        at0 = NRING * (EWG + EWD)
        xg = big[:, at0:at0 + PAIRS * XW].rearrange("p (j w) -> p j w", j=PAIRS)
        at0 += PAIRS * XW
        xgt = big[:, at0:at0 + 2 * H].rearrange("p (n k c) -> p n k c", n=2, k=HK)
        at0 += 2 * H
        egu = big[:, at0:at0 + 4 * I].rearrange("p (n f) -> p n f", n=4)
        at0 += 4 * I
        eat = big[:, at0:at0 + 2 * H].rearrange("p (n k c) -> p n k c", n=2, k=2)
        at0 += 2 * H
        ey = big[:, at0:at0 + 2 * H].rearrange("p (n o) -> p n o", n=2)
        at0 += 2 * H
        assert at0 <= QSB + KSB + PTB, (at0, QSB + KSB + PTB)

        d_x = [sem(f"d_x{b}") for b in range(NB)]
        d_c0, d_c1 = sem("d_c0"), sem("d_c1")
        d_wqkv, d_wsh = sem("d_wqkv"), sem("d_wsh")
        d_ew = [sem(f"d_ew{n}") for n in range(NOWN + NEARLY + NRING)]
        d_part = [sem("d_part0"), sem("d_part1")]
        d_stack = [sem("d_stack0"), sem("d_stack1")]
        d_mrow = [sem("d_mrow0"), sem("d_mrow1")]
        d_scr, d_zero, d_merge = sem("d_scr"), sem("d_zero"), sem("d_merge")
        d_gather, d_plane = [sem(f"d_gather{j}") for j in range(PAIRS)], sem("d_plane")
        d_fin, d_out = [sem(f"d_fin{n}") for n in range(4)], sem("d_out")
        s_const, s_dve, s_pool = sem("s_const"), sem("s_dve"), sem("s_pool")
        s_p1, s_max = sem("s_p1"), sem("s_max")
        s_p2, s_exp = sem("s_p2"), sem("s_exp")
        s_av, s_out = sem("s_av"), sem("s_out")
        m_full = [sem("m_full0"), sem("m_full1")]
        m_taken = [sem("m_taken0"), sem("m_taken1")]
        s_var, s_rstd, s_xn = sem("s_var"), sem("s_rstd"), sem("s_xn")
        s_roped, s_hi, s_res, s_mid, s_lo = ([sem(f"s_{n}{c}") for c in range(3)]
                                             for n in ("roped", "hi", "res", "mid", "lo"))
        s_mrow, s_tanh, s_keys = sem("s_mrow"), sem("s_tanh"), sem("s_keys")
        s_mask, s_ex, s_sel, s_row = sem("s_mask"), sem("s_ex"), sem("s_sel"), sem("s_row")
        s_best, s_tk, s_idx, s_ws = sem("s_best"), sem("s_tk"), sem("s_idx"), sem("s_ws")
        s_pad0, s_pad1, s_fin = sem("s_pad0"), sem("s_pad1"), sem("s_fin")
        e_xt, e_xtc, e_gu, e_th = sem("e_xt"), sem("e_xtc"), sem("e_gu"), sem("e_th")
        e_act, e_at, e_atc, e_dn, e_y = sem("e_act"), sem("e_at"), sem("e_atc"), sem("e_dn"), sem("e_y")
        RING = [(e % (NOWN + NEARLY + NRING), e // (NOWN + NEARLY + NRING)) for e in range(E)]

        def bank(p):
            return ps_m[:, PLACE[p] % 2, :]

        def wait_bank(eng, p):
            n = PLACE[p]
            if n >= 2:
                eng.wait_ge(m_taken[n % 2], n // 2)

        def wait_product(eng, p):
            eng.wait_ge(m_full[PLACE[p] % 2], PLACE[p] // 2 + 1)

        def full(p):
            return m_full[PLACE[p] % 2]

        def taken(p):
            return m_taken[PLACE[p] % 2]

        def wait_taken(eng, p):
            eng.wait_ge(m_taken[PLACE[p] % 2], PLACE[p] // 2 + 1)

        block = ctx.enter_context(nc.Block())

        @block.sync
        def _(sp):
            for b in range(NB):
                sp.dma_start(xs[:, NT * b:NT * b + NT, :],
                             x[S * b:S * b + S, :].rearrange("(i p) h -> p i h", p=P)).then_inc(d_x[b], 16)
                if b == 0:
                    sp.dma_start(ident[:, :], ident_in).then_inc(d_c0, 16)
                    sp.dma_start(wq_s[:, :, :], wq.rearrange("(k p) o -> p k o", p=P)).then_inc(d_wqkv, 16)
                    sp.dma_start(wkv_s[:, :, :], wkv.rearrange("(k p) o -> p k o", p=P)).then_inc(d_wqkv, 16)
                    sp.dma_start(cos_s[:, :], cosr).then_inc(d_c0, 16)
                    sp.dma_start(sin_s[:, :], sinr).then_inc(d_c0, 16)

            def stack_out(b):
                q = b % 2
                for c in range(3):
                    sp.wait_ge(s_lo[c], b + 1)
                if b >= 2:
                    sp.wait_ge(d_stack[q], 16 * 12 * (b // 2))
                for j in range(3):
                    for m in range(2):
                        sp.dma_start(q_scr[q, j, P * m:P * m + P, :], part[:, j, m, :]).then_inc(d_part[q], 16)
                    sp.dma_start(k_scr[q, j, :, :], part[0:NKV * HD, j, 2, :]).then_inc(d_part[q], 16)

            def stack_in(b):
                q = b % 2
                sp.wait_ge(d_part[q], 16 * 9 * (b // 2 + 1))
                if b >= 2:
                    sp.wait_ge(s_p2, 64 * (b - 1))
                for r in range(6):
                    sp.dma_start(qs[16 * r:16 * r + 16, q, :, :],
                                 q_scr[q, QPART[r]].rearrange("(h d) s -> d h s", d=HD)).then_inc(d_stack[q], 16)
                    sp.dma_start(ks[16 * r:16 * r + 16, q, :, :],
                                 k_scr[q, KPART[r]].rearrange("(h d) s -> d h s", d=HD)).then_inc(d_stack[q], 16)

            def weights(e):
                n, turn = RING[e]
                if turn >= 1:
                    sp.wait_ge(e_dn, (e - (NOWN + NEARLY + NRING)) // 2 + 1)
                t = ew[n]
                sp.dma_start(t[:, 0:EWG].rearrange("p (k f) -> p k f", k=HK),
                             wgu[e].rearrange("(k p) f -> p k f", p=P)).then_inc(d_ew[n], 16)
                sp.dma_start(t[:, EWG:EWG + H], wd[e, 0:P, :]).then_inc(d_ew[n], 16)
                sp.dma_start(t[0:I - P, EWG + H:EWG + EWD], wd[e, P:I, :]).then_inc(d_ew[n], 16)

            sp.wait_ge(s_const, 1)
            stack_out(0)
            stack_in(0)
            sp.dma_start(wo_s[:, :, :], wo.rearrange("(k p) o -> p k o", p=P)).then_inc(d_c1, 16)
            sp.dma_start(gate_s[:, :, :], gate.rearrange("(k p) o -> p k o", p=P)).then_inc(d_c1, 16)
            sp.dma_start(keys[:, :, :], keys_in).then_inc(d_c1, 16)
            sp.dma_start(tri[:, :, :], tri_in).then_inc(d_c1, 16)
            sp.dma_start(emask[:, :, :], emask_in).then_inc(d_c1, 16)
            sp.dma_start(pad[:, :], pad_in).then_inc(d_c1, 16)
            sp.dma_start(wsgu_s[:, :, :], wsgu.rearrange("(k p) o -> p k o", p=P)).then_inc(d_wsh, 16)
            sp.dma_start(wsd_s[:, 0:2, :], wsd[0:2 * P, :].rearrange("(k p) o -> p k o", p=P)).then_inc(d_wsh, 16)
            sp.dma_start(wsd_s[0:ISH - 2 * P, 2, :], wsd[2 * P:ISH, :]).then_inc(d_wsh, 16)
            sp.dma_start(x_scr[T:ROWS, :], zero[:, :]).then_inc(d_scr, 16)
            for t in range(END + 1):
                for name, b in products_at(t - 1):
                    if name == "MT":
                        g, q = b % NKV, b // NKV % 2
                        sp.wait_ge(s_mrow, b + 1)
                        if b >= 8:
                            sp.wait_ge(s_p2, 16 * (b - 7))
                        for j in range(3):
                            sp.dma_start(qs[MROW + j:MROW + j + 1, q, REP * g:REP * g + REP, :]
                                         .rearrange("o h (i p) -> o (h i) p", p=P),
                                         mrow[0:16, b % 2, j, :]).then_inc(d_mrow[b % 2], 16)
                    if name == "ST":
                        sp.wait_ge(s_row, b + 1)
                        sp.dma_start(x_scr[S * b:S * b + S, :].rearrange("(i p) w -> p i w", p=P),
                                     xr[:, :, :]).then_inc(d_scr, 16)
                        if b == NB - 1:
                            sp.wait_ge(s_best, NB)
                            for i in range(NT):
                                sp.dma_start(merged[:, C * i:C * i + C],
                                             best[E * i:E * i + E, :]).then_inc(d_merge, 16)
                if t % 64 == STACK_OUT and t // 64 + 1 < NB:
                    stack_out(t // 64 + 1)
                if t % 64 == STACK_IN and t // 64 + 1 < NB:
                    stack_in(t // 64 + 1)
                if t < 16 * NOWN and t % 16 == 8:
                    weights(t // 16)
                if t % 8 == 3 and t // 8 < 2 * ROWS // P:
                    n = t // 8
                    sp.dma_start(plane[P * n:P * n + P, :], zero[:, 0:H]).then_inc(d_zero, 16)
                if t == FREE_EARLY + 4:
                    sp.wait_ge(s_pad0, 1)
                if FREE_EARLY + 4 <= t < FREE_EARLY + 4 + 8 * NEARLY and (t - FREE_EARLY) % 8 == 4:
                    weights(NOWN + (t - FREE_EARLY) // 8)
                if t == FREE_ALL + 2:
                    sp.wait_ge(s_pad1, 1)
                    for e in range(NOWN + NEARLY, NOWN + NEARLY + NRING):
                        weights(e)
            for e in range(NOWN + NEARLY + NRING, E):
                weights(e)
            sp.wait_ge(d_plane, 16 * PAIRS)
            for n in range(NB * 2):
                q = n % 4
                if n >= 4:
                    sp.wait_ge(s_fin, n - 3)
                for half in range(2):
                    sp.dma_start(fin[:, q, half, :, :],
                                 plane[ROWS * half + 2 * P * n:ROWS * half + 2 * P * n + 2 * P, :]
                                 .rearrange("(i p) h -> p i h", p=P)).then_inc(d_fin[q], 16)
            sp.wait_ge(d_out, 16 * NB * 2)

        @block.tensor
        def _(pe):
            def product(p, part=0, parts=1):
                name, b = p
                first, last = part == 0, part == parts - 1
                if name in ("T0", "T1"):
                    k = int(name[1])
                    if p == ORDER[0]:
                        pe.wait_ge(d_c0, 16 * 3)
                    pe.wait_ge(s_xn, NORM_AT[0, b])
                    wait_bank(pe, p)
                    for i in range(NT):
                        mm = pe.transpose(bank(p)[:, P * i:P * i + P], xn[:, i, P * k:P * k + P], ident[:, :])
                elif name in ("Q0", "Q1", "KV"):
                    if name == "Q0" and first:
                        if b == 0:
                            pe.wait_ge(d_wqkv, 32)
                        wait_taken(pe, ("T0", b))
                        wait_taken(pe, ("T1", b))
                    w = wkv_s[:, :, :] if name == "KV" else wq_s[:, :, P * int(name[1]):P * int(name[1]) + P]
                    if first:
                        wait_bank(pe, p)
                    for k in range(HK)[part::parts]:
                        mm = pe.matmul(bank(p), w[:, k, :], xt[:, k, :], start=(k == 0), stop=(k == HK - 1))
                elif name == "VT":
                    wait_taken(pe, ("KV", b))
                    wait_bank(pe, p)
                    for i in range(NT):
                        mm = pe.transpose(bank(p)[:, 64 * i:64 * i + 64], vt[64:P, P * i:P * i + P],
                                          ident[64:P, 64:P])
                elif name == "MT":
                    pe.wait_ge(s_max, 16 * (b + 1))
                    wait_bank(pe, p)
                    mm = pe.transpose(bank(p)[0:16, 0:P], mx[:, b % 2, :], ident[:, :])
                elif name == "NT":
                    pe.wait_ge(s_out, b + 1)
                    wait_bank(pe, p)
                    for i in range(NT):
                        mm = pe.transpose(bank(p)[:, P * i:P * i + P], osb[:, P * i:P * i + P], ident[:, :])
                elif name in ("OT0", "OT1"):
                    k = int(name[2])
                    wait_taken(pe, ("NT", NKV * b + NKV - 1))
                    wait_bank(pe, p)
                    for i in range(NT):
                        mm = pe.transpose(bank(p)[:, P * i:P * i + P], od[:, i, P * k:P * k + P], ident[:, :])
                elif name in ("W0", "W1"):
                    if name == "W0" and first:
                        wait_taken(pe, ("OT0", b))
                        wait_taken(pe, ("OT1", b))
                        if b == 0:
                            pe.wait_ge(d_c1, 16 * 6)
                    if first:
                        wait_bank(pe, p)
                    for n in range(2)[part::parts]:
                        i = 2 * int(name[1]) + n
                        for k in range(HK):
                            mm = pe.matmul(bank(p)[:, H * n:H * n + H], ot[:, k, P * i:P * i + P], wo_s[:, k, :],
                                           start=(k == 0), stop=(k == HK - 1))
                elif name in ("U0", "U1"):
                    k = int(name[1])
                    pe.wait_ge(s_xn, NORM_AT[1, b])
                    wait_bank(pe, p)
                    for i in range(NT):
                        mm = pe.transpose(bank(p)[:, P * i:P * i + P], xr[:, i, P * k:P * k + P], ident[:, :])
                elif name == "GL":
                    wait_taken(pe, ("U0", b))
                    wait_taken(pe, ("U1", b))
                    wait_bank(pe, p)
                    for k in range(HK):
                        for i in range(NT):
                            mm = pe.matmul(bank(p)[E * i:E * i + E, 0:P], gate_s[:, k, :], xrt[:, k, P * i:P * i + P],
                                           start=(k == 0), stop=(k == HK - 1), skip_group_check=True)
                elif name == "GT":
                    wait_taken(pe, ("GL", b))
                    wait_bank(pe, p)
                    mm = pe.transpose(bank(p)[:, 0:P], lgt[:, :], ident[:, :])
                elif name == "ST":
                    pe.wait_ge(s_sel, b + 1)
                    wait_bank(pe, p)
                    mm = pe.transpose(bank(p)[:, 0:P], sel[:, :, :], ident[:, :])
                elif name == "KP":
                    pe.wait_ge(s_tk, 1)
                    wait_bank(pe, p)
                    for half in range(2):
                        mm = pe.matmul(bank(p)[64 * half:64 * half + 64, 0:PAIRS], best2[:, :],
                                       ident[0:E, half:E:2], start=True, stop=True, skip_group_check=True)
                elif name[0] == "A":
                    c, up = int(name[1]) // 2, int(name[1]) % 2
                    m = min(P, ISH - P * c)
                    if p == ("A0", 0) and first:
                        pe.wait_ge(d_wsh, 16 * 3)
                    if first:
                        wait_bank(pe, p)
                    for k in range(HK)[part::parts]:
                        mm = pe.matmul(bank(p)[0:m, :], wsgu_s[:, k, ISH * up + P * c:ISH * up + P * c + m],
                                       xrt[:, k, :], start=(k == 0), stop=(k == HK - 1))
                else:
                    if first:
                        wait_taken(pe, ("A5", b))
                        wait_bank(pe, p)
                    for m in range(6)[2 * part:2 * part + 2]:
                        n, c = m // 3, m % 3
                        i = 2 * int(name[1]) + n
                        mm = pe.matmul(bank(p)[:, H * n:H * n + H], hs[:, c, P * i:P * i + P], wsd_s[:, c, :],
                                       start=(c == 0), stop=(c == 2))
                if last:
                    mm.then_inc(full(p), 1)

            for name in PROLOGUE:
                product((name, 0))
            for t in range(END):
                if t < UNITS:
                    s, hl, i = t // 16, t // 4 % 4, t % 4
                    b, g = s // NKV, s % NKV
                    if s % NKV == 0 and t % 16 == 0:
                        pe.wait_ge(d_stack[b % 2], 16 * 12 * (b // 2 + 1))
                    if t >= 2:
                        pe.wait_ge(s_max, t - 1)
                    pe.matmul(score[t % 2][:, 0, :], qs[0:MROW, b % 2, REP * g + hl, P * i:P * i + P],
                              ks[0:MROW, b % 2, g, :], start=True, stop=True).then_inc(s_p1, 1)
                v = t - LAG
                if 0 <= v < UNITS:
                    s, kt, hl = v // 16, v // 4 % 4, v % 4
                    b, g = s // NKV, s % NKV
                    if v % 16 == 0:
                        pe.wait_ge(d_mrow[s % 2], 16 * 3 * (s // 2 + 1))
                    if v >= NS:
                        pe.wait_ge(s_exp, v - NS + 1)
                    pe.matmul(ps_s[:, v % NS, :], ks[0:KR, b % 2, g, P * kt:P * kt + P],
                              qs[0:KR, b % 2, REP * g + hl, :], start=True, stop=True).then_inc(s_p2, 1)
                if 0 <= t - AVLAG < UNITS and (t - AVLAG) % 4 == 0:
                    n = (t - AVLAG) // 4
                    s, kt = n // 4, n % 4
                    pe.wait_ge(s_exp, 4 * n + 4)
                    if kt == 0 and s >= 1:
                        pe.wait_ge(s_out, s)
                    if kt == 0 and s % NKV == 0:
                        wait_taken(pe, ("VT", s // NKV))
                    for hl in range(REP):
                        mm = pe.matmul(ps_o[32 * hl:32 * hl + 32, 0, :], vs[:, s // NKV % 2, kt, s % NKV, :],
                                       pt[:, n % NP, hl, :], start=(kt == 0), stop=(kt == 3), skip_group_check=True)
                    mm.then_inc(s_av, 1)
                for p, n, parts in parts_at(t):
                    product(p, n, parts)

            def x_turn(j):
                pe.wait_ge(d_gather[j], 16)
                if j >= 2:
                    pe.wait_ge(e_xtc, j - 1)
                for k in range(HK):
                    mm = pe.transpose(score[j % 2][:, 0, P * k:P * k + P], xg[:, j, P * k:P * k + P], ident[:, :])
                mm.then_inc(e_xt, 1)

            def gate_up(j):
                pe.wait_ge(e_xtc, j + 1)
                if j >= 2:
                    pe.wait_ge(e_act, j - 1)
                for half in range(2):
                    slot, turn = RING[2 * j + half]
                    pe.wait_ge(d_ew[slot], 48 * (turn + 1))
                for k in range(HK):
                    for half in range(2):
                        w = ew[RING[2 * j + half][0]]
                        mm = pe.matmul(ps_s[64 * half:64 * half + 64, j % 2, 0:2 * I],
                                       xgt[:, j % 2, k, 64 * half:64 * half + 64],
                                       w[:, 2 * I * k:2 * I * k + 2 * I],
                                       start=(k == 0), stop=(k == HK - 1), skip_group_check=True)
                mm.then_inc(e_gu, 1)

            def act_turn(j):
                pe.wait_ge(e_act, j + 1)
                if j >= 1:
                    pe.wait_ge(e_atc, j)
                pe.transpose(ps_o[:, 0, 0:P], egu[:, 2 + j % 2, 0:P], ident[:, :])
                pe.transpose(ps_o[0:I - P, 0, P:2 * P], egu[:, 2 + j % 2, P:I], ident[:, :]).then_inc(e_at, 1)

            def down(j):
                pe.wait_ge(e_atc, j + 1)
                if j >= 2:
                    pe.wait_ge(e_y, j - 1)
                for k in range(2):
                    for half in range(2):
                        w = ew[RING[2 * j + half][0]]
                        mm = pe.matmul(ps_m[64 * half:64 * half + 64, j % 2, 0:H],
                                       eat[:, j % 2, k, 64 * half:64 * half + 64],
                                       w[:, EWG + H * k:EWG + H * k + H],
                                       start=(k == 0), stop=(k == 1), skip_group_check=True)
                mm.then_inc(e_dn, 1)

            for n in range(len(ORDER) - 2, len(ORDER)):
                wait_taken(pe, ORDER[n])
            for j in range(-2, PAIRS):
                if j + 2 < PAIRS:
                    x_turn(j + 2)
                if 0 <= j + 1 < PAIRS:
                    gate_up(j + 1)
                if j >= 0:
                    act_turn(j)
                    down(j)

        @block.scalar
        def _(act):
            def consume(p):
                name, b = p
                if name in ("T0", "T1", "U0", "U1"):
                    dst = (xt if name[0] == "T" else xrt)[:, int(name[1]), :]
                    wait_product(act, p)
                    if name == "T0" and b > 0:
                        wait_product(act, ("KV", b - 1))
                    if name == "U0" and b > 0:
                        wait_product(act, ("A5", b - 1))
                    nc.scalar.activation(dst, bank(p), ACT.Copy).then_inc(taken(p), 1)
                if name in ("OT0", "OT1"):
                    wait_product(act, p)
                    if name == "OT0" and b > 0:
                        wait_product(act, ("W1", b - 1))
                    nc.scalar.activation(ot[:, int(name[2]), :], bank(p), ACT.Copy).then_inc(taken(p), 1)
                if name == "KV":
                    wait_product(act, p)
                    act.wait_ge(s_keys, b + 1)
                    if b > 0:
                        wait_product(act, ("VT", b - 1))
                    nc.scalar.activation(vt[64:P, :], bank(p)[64:P, :], ACT.Copy).then_inc(taken(p), 1)
                if name == "VT":
                    wait_product(act, p)
                    if b >= 2:
                        act.wait_ge(s_av, 16 * (b - 1))
                    nc.scalar.activation(vs[:, b % 2, :, :, 0:HD],
                                         bank(p)[:, 0:NT * NKV * HD].rearrange("p (i g d) -> p i g d", i=NT, g=NKV),
                                         ACT.Copy).then_inc(taken(p), 1)
                if name == "GL":
                    wait_product(act, p)
                    nc.scalar.activation(lgt[:, :], bank(p)[:, 0:P], ACT.Copy).then_inc(taken(p), 1)
                if name in ("A1", "A3", "A5"):
                    c = int(name[1]) // 2
                    g = (f"A{2 * c}", b)
                    m = min(P, ISH - P * c)
                    wait_product(act, g)
                    if (c, b) != (0, 0):
                        wait_taken(act, (f"A{2 * c - 1}", b) if c else ("A5", b - 1))
                    nc.scalar.activation(th[0:m, :], bank(g)[0:m, :], ACT.Tanh, scale=0.5).then_inc(s_tanh, 1)

            def gate_exp(b):
                act.wait_ge(s_mask, b + 1)
                nc.scalar.activation(ex[:, :, :], lg[:, :, :], ACT.Exp).then_inc(s_ex, 1)

            def high(p):
                c = ("Q0", "Q1", "KV").index(p[0])
                m = P if c < 2 else NKV * HD
                act.wait_ge(s_roped[c], p[1] + 1)
                if p[1] > 0:
                    act.wait_ge(d_part[(p[1] - 1) % 2], 16 * 9 * ((p[1] - 1) // 2 + 1))
                nc.scalar.activation(part[0:m, 0, c, :], qa[0:m, c, :], ACT.Copy).then_inc(s_hi[c], 1)

            def middle(p):
                c = ("Q0", "Q1", "KV").index(p[0])
                m = P if c < 2 else NKV * HD
                act.wait_ge(s_res[c], p[1] + 1)
                nc.scalar.activation(part[0:m, 1, c, :], qa[0:m, c, :], ACT.Copy).then_inc(s_mid[c], 1)

            for name in PROLOGUE[:5]:
                consume((name, 0))
            for name in ("Q0", "Q1", "KV"):
                high((name, 0))
                middle((name, 0))
            consume(("VT", 0))
            for t in range(END + 1):
                v = t - LAG
                if 0 <= v < UNITS:
                    n, hl = v // 4, v % 4
                    act.wait_ge(s_p2, v + 1)
                    if n >= NP and hl == 0:
                        act.wait_ge(s_av, n - NP + 1)
                    nc.scalar.activation(pt[:, n % NP, hl, :], ps_s[:, v % NS, :], ACT.Exp,
                                         scale=ATT_SCALE).then_inc(s_exp, 1)
                for p in products_at(t - 1):
                    consume(p)
                for p in products_at(t - 4):
                    if p[0] in ("Q0", "Q1", "KV"):
                        high(p)
                for p in products_at(t - 6):
                    if p[0] in ("Q0", "Q1", "KV"):
                        middle(p)
                for p in products_at(t - 8):
                    if p[0] == "GT":
                        gate_exp(p[1])
                if (t - AVLAG - 13) % 16 == 0 and 0 <= (t - AVLAG - 13) // 16 < STEPS:
                    s = (t - AVLAG - 13) // 16
                    act.wait_ge(s_av, 4 * s + 4)
                    if s >= 1:
                        wait_product(act, ("NT", s - 1))
                    nc.scalar.activation(osb[:, :], ps_o[:, 0, :], ACT.Copy).then_inc(s_out, 1)
            for j in range(-2, PAIRS):
                if j + 2 < PAIRS:
                    n = j + 2
                    act.wait_ge(e_xt, n + 1)
                    if n >= 2:
                        act.wait_ge(e_gu, n - 1)
                    nc.scalar.activation(xgt[:, n % 2, :, :], score[n % 2][:, 0, 0:H].rearrange("p (k c) -> p k c", k=HK),
                                         ACT.Copy).then_inc(e_xtc, 1)
                if 0 <= j + 1 < PAIRS:
                    n = j + 1
                    act.wait_ge(e_gu, n + 1)
                    if n >= 2:
                        act.wait_ge(e_act, n - 1)
                    nc.scalar.activation(egu[:, n % 2, :], ps_s[:, n % 2, 0:I], ACT.Tanh, scale=0.5).then_inc(e_th, 1)
                if j >= 0:
                    act.wait_ge(e_dn, j + 1)
                    act.wait_ge(s_ws, j + 1)
                    if j >= 2:
                        act.wait_ge(d_plane, 16 * (j - 1))
                    nc.scalar.activation(ey[:, j % 2, :], ps_m[:, j % 2, 0:H], ACT.Copy,
                                         scale=wslot[:, j:j + 1]).then_inc(e_y, 1)
            for n in range(NB * 2):
                act.wait_ge(s_fin, n + 1)
                act.dma_start(out[2 * P * n:2 * P * n + 2 * P, :].rearrange("(i p) h -> p i h", p=P),
                              xs[:, 2 * n:2 * n + 2, :]).then_inc(d_out, 16)

        @block.gpsimd
        def _(pool):
            count = [0]

            def link(ins):
                count[0] += 1
                ins.then_inc(s_pool, 1)
                pool.wait_ge(s_pool, count[0])

            def rope(p):
                name, b = p
                c = ("Q0", "Q1", "KV").index(name)
                m = P if c < 2 else NKV * HD
                if c == 2:
                    pool.wait_ge(s_keys, b + 1)
                else:
                    wait_taken(pool, p)
                g = nc.gpsimd
                link(g.tensor_tensor(qb[0:m, c, :], qb[0:m, c, :], sin_s[0:m, :], ALU.mult))
                g.tensor_tensor(qa[0:m, c, :], qa[0:m, c, :], qb[0:m, c, :], ALU.add).then_inc(s_roped[c], 1)
                pool.wait_ge(s_roped[c], b + 1)
                pool.wait_ge(s_hi[c], b + 1)
                g.tensor_tensor(qa[0:m, c, :], qa[0:m, c, :], part[0:m, 0, c, :], ALU.subtract).then_inc(s_res[c], 1)
                pool.wait_ge(s_res[c], b + 1)
                pool.wait_ge(s_mid[c], b + 1)
                g.tensor_tensor(part[0:m, 2, c, :], qa[0:m, c, :], part[0:m, 1, c, :],
                                ALU.subtract).then_inc(s_lo[c], 1)

            def root(n, which):
                pool.wait_ge(s_var, n)
                nc.gpsimd.tensor_tensor(rstd[:, which, :], rstd[:, which, :], halfs[:, :], ALU.pow).then_inc(s_rstd, 1)

            root(1, 0)
            rope(("KV", 0))
            for t in range(END + 1):
                for kind, bb in norms_at(t):
                    root(NORM_AT[kind, bb], kind)
                for p in products_at(t - 1):
                    if p[0] in ("Q0", "Q1", "KV"):
                        rope(p)
            pool.wait_ge(s_idx, 2)
            pool.wait_ge(d_scr, 16 * (NB + 1))
            pool.wait_ge(s_pad1, 1)
            for j in range(PAIRS):
                nc.gpsimd.indirect_dma_start(out=xg[:, j, :], out_offset=None, in_=x_scr,
                                             in_offset=bass.IndirectOffsetOnAxis(ap=idx[:, 0, j:j + 1], axis=0),
                                             ).then_inc(d_gather[j], 16)
            pool.wait_ge(d_zero, 16 * (2 * ROWS // P))
            for j in range(PAIRS):
                pool.wait_ge(e_y, j + 1)
                if j >= 1:
                    pool.wait_ge(d_plane, 16 * j)
                nc.gpsimd.indirect_dma_start(out=plane, in_=ey[:, j % 2, :], in_offset=None,
                                             out_offset=bass.IndirectOffsetOnAxis(ap=idx[:, 1, j:j + 1], axis=0),
                                             compute_op=ALU.add).then_inc(d_plane, 16)
            pool.wait_ge(d_plane, 16 * PAIRS)

        @block.vector
        def _(dve):
            count = [0]

            def link(ins):
                count[0] += 1
                ins.then_inc(s_dve, 1)
                dve.wait_ge(s_dve, count[0])

            V = nc.vector
            for tile in (zero, cand, best2):
                V.memset(tile[:], 0.0)
            V.memset(wsd_s[ISH - 2 * P:P, 2, :], 0.0)
            V.memset(hs[ISH - 2 * P:P, 2, :], 0.0)
            for n in range(NOWN):
                V.memset(ew[n][:, EWG + H:EWG + EWD], 0.0)
            V.memset(halfs[:], -0.5)
            V.memset(ks[MROW:P, :, :, :], 1.0)
            V.memset(vs[:, :, :, :, HD:2 * HD], 1.0).then_inc(s_const, 1)
            dve.wait_ge(s_const, 1)

            def norm_stats(src, which):
                for i in range(NT):
                    ins = V.bn_stats(stat[:, which, i, :], src(i))
                link(ins)
                for i in range(NT):
                    ins = V.bn_aggr(agg[:, which, i, :], stat[:, which, i, :])
                link(ins)
                V.tensor_scalar(rstd[:, which, :], agg[:, which, :, 1], EPS, None, ALU.add).then_inc(s_var, 1)

            def norm_apply(src, dst, which, n):
                dve.wait_ge(s_rstd, n)
                for i in range(NT):
                    ins = V.tensor_scalar(dst(i), src(i), agg[:, which, i, 0:1], rstd[:, which, i:i + 1],
                                          ALU.subtract, ALU.mult)
                ins.then_inc(s_xn, 1)

            def stats(kind, b):
                if kind == 0:
                    dve.wait_ge(d_x[b], 16)
                norm_stats(lambda i: xs[:, NT * b + i, :], kind)

            def apply(kind, b):
                if kind == 0:
                    if b > 0:
                        wait_product(dve, ("T1", b - 1))
                        wait_product(dve, ("T0", b - 1))
                    norm_apply(lambda i: xs[:, NT * b + i, :], lambda i: xn[:, i, :], 0, NORM_AT[0, b])
                else:
                    if b > 0:
                        dve.wait_ge(d_scr, 16 * (b + 1))
                    norm_apply(lambda i: xs[:, NT * b + i, :], lambda i: xr[:, i, 0:H], 1, NORM_AT[1, b])

            def route(b, p):
                wait_product(dve, p)
                V.tensor_copy(lg[:, :, :], bank(p)[:, 0:P].rearrange("p (i e) -> p i e", i=NT)).then_inc(taken(p), 1)
                wait_taken(dve, p)
                link(V.tensor_reduce(gs[:, :, :], lg[:, :, :].rearrange("p i (g e) -> p (i g) e", g=G), AX.X, ALU.max))
                for i in range(NT):
                    mine = gs[:, i, :, None].broadcast_to([P, G, G])
                    other = gs[:, i, None, :].broadcast_to([P, G, G])
                    V.tensor_tensor(cmp[:, i, :, :], other, mine, ALU.is_gt)
                    ins = V.tensor_tensor(eq[:, i, :, :], other, mine, ALU.is_equal)
                link(ins)
                for i in range(NT):
                    ins = V.tensor_tensor(eq[:, i, :, :], eq[:, i, :, :], tri[:, :, :], ALU.mult)
                link(ins)
                link(V.tensor_tensor(cmp[:, :, :, :], cmp[:, :, :, :], eq[:, :, :, :], ALU.add))
                link(V.tensor_reduce(rank[:, :, :], cmp[:, :, :, :].rearrange("p i a c -> p (i a) c"), AX.X, ALU.add))
                link(V.tensor_scalar(rank[:, :, :], rank[:, :, :], TG - 0.5, None, ALU.is_lt))
                keep = rank[:, :, :].rearrange("p i g -> p (i g)")[:, :, None].broadcast_to([P, NT * G, EG])
                lgv = lg[:, :, :].rearrange("p i (g e) -> p (i g) e", g=G)
                link(V.tensor_tensor(lgv, lgv, keep, ALU.mult))
                link(V.tensor_reduce(exs[:, :, 0], lg[:, :, :], AX.X, ALU.max))
                V.tensor_tensor(lg[:, :, :], lg[:, :, :], exs[:, :, 0:1].broadcast_to([P, NT, E]),
                                ALU.subtract).then_inc(s_mask, 1)

            def choose(b):
                dve.wait_ge(s_ex, b + 1)
                V.tensor_reduce(exs[:, :, 1], ex[:, :, :], AX.X, ALU.add)
                for i in range(NT):
                    ins = V.max(top[:, i, :], ex[:, i, :])
                link(ins)
                V.reciprocal(exs[:, :, 2:3], exs[:, :, 1:2])
                link(V.memset(top[:, :, TOPK:8], -5.0))
                for i in range(NT):
                    ins = V.match_replace(out=rep[:, i, :], in_to_replace=top[:, i, :], in_values=ex[:, i, :],
                                          imm_value=-1.0)
                link(ins)
                link(V.tensor_scalar(exs[:, :, 3:4], exs[:, :, 2:3], SCALE_W, None, ALU.mult))
                V.tensor_scalar(sel[:, :, :], rep[:, :, :], 0.0, None, ALU.is_lt).then_inc(s_sel, 1)
                V.tensor_tensor(xr[:, :, H:XW], ex[:, :, :], exs[:, :, 3:4].broadcast_to([P, NT, E]),
                                ALU.mult).then_inc(s_row, 1)

            def best_keys(src, dst, n, done):
                for r in range(n // 8):
                    if r:
                        link(V.match_replace(out=src, in_to_replace=dst[:, 8 * r - 8:8 * r], in_values=src,
                                             imm_value=0.0))
                    ins = V.max(dst[:, 8 * r:8 * r + 8], src)
                    if r == n // 8 - 1:
                        done(ins)
                    else:
                        link(ins)

            def consume(p):
                name, b = p
                if name in ("Q0", "Q1", "KV"):
                    c = ("Q0", "Q1", "KV").index(name)
                    n = 3 * b + c
                    m = P if c < 2 else NKV * HD
                    wait_product(dve, p)
                    if p == ("Q0", 0):
                        dve.wait_ge(d_c0, 48)
                    if b > 0:
                        dve.wait_ge(s_lo[c], b)
                    V.stream_shuffle(qb[0:m, c, :], bank(p)[0:m, :], [i ^ 8 for i in range(32)])
                    V.tensor_tensor(qa[0:m, c, :], bank(p)[0:m, :], cos_s[0:m, :],
                                    ALU.mult).then_inc(s_keys if c == 2 else taken(p), 1)
                if name == "NT":
                    wait_product(dve, p)
                    if b >= 1:
                        wait_taken(dve, ("NT", b - 1))
                    if b % NKV == 0 and b > 0:
                        wait_product(dve, ("OT1", b // NKV - 1))
                    o = bank(p).rearrange("p (i h d) -> p i h d", i=NT, h=REP)
                    link(V.reciprocal(rec[:, :, :], o[:, :, :, HD]))
                    g = b % NKV
                    V.tensor_tensor(od[:, :, 64 * g:64 * g + 64].rearrange("p i (h d) -> p i h d", h=REP),
                                    o[:, :, :, 0:HD], rec[:, :, :, None].broadcast_to([P, NT, REP, HD]),
                                    ALU.mult).then_inc(taken(p), 1)
                if name == "MT":
                    wait_product(dve, p)
                    if b >= 2:
                        dve.wait_ge(d_mrow[b % 2], 48 * (b // 2))
                    row = mrow[:, b % 2, :, :]
                    link(V.tensor_scalar(row[:, 0, :], bank(p)[0:16, 0:P], -1.0, None, ALU.mult))
                    link(V.scalar_tensor_tensor(out=mr[:, :], in0=bank(p)[0:16, 0:P], scalar=-1.0, in1=row[:, 0, :],
                                                op0=ALU.mult, op1=ALU.subtract))
                    V.tensor_copy(row[:, 1, :], mr[:, :]).then_inc(taken(p), 1)
                    wait_taken(dve, p)
                    V.tensor_tensor(row[:, 2, :], mr[:, :], row[:, 1, :], ALU.subtract).then_inc(s_mrow, 1)
                if name in ("W0", "W1", "D0", "D1"):
                    i = NT * b + 2 * int(name[1])
                    wait_product(dve, p)
                    V.tensor_tensor(xs[:, i:i + 2, :], xs[:, i:i + 2, :],
                                    bank(p).rearrange("p (n h) -> p n h", n=2), ALU.add).then_inc(taken(p), 1)
                    wait_taken(dve, p)
                if name == "GT":
                    route(b, p)
                if name in ("A1", "A3", "A5"):
                    c = int(name[1]) // 2
                    g = (f"A{2 * c}", b)
                    m = min(P, ISH - P * c)
                    dve.wait_ge(s_tanh, 3 * b + c + 1)
                    wait_product(dve, p)
                    if c == 0 and b > 0:
                        wait_product(dve, ("D1", b - 1))
                    V.scalar_tensor_tensor(out=hs[0:m, c, :], in0=th[0:m, :], scalar=1.0, in1=bank(g)[0:m, :],
                                           op0=ALU.add, op1=ALU.mult).then_inc(taken(g), 1)
                    wait_taken(dve, g)
                    V.scalar_tensor_tensor(out=hs[0:m, c, :], in0=hs[0:m, c, :], scalar=0.5, in1=bank(p)[0:m, :],
                                           op0=ALU.mult, op1=ALU.mult).then_inc(taken(p), 1)
                if name == "KP":
                    wait_product(dve, p)
                    keyp = bank(p)[:, 0:PAIRS]
                    V.tensor_scalar(idz[:, :], keyp, 0.0, pad[:, 0:1], ALU.is_equal, ALU.mult)
                    V.tensor_scalar(idf[:, :], keyp, -1.0, float(T), ALU.mult, ALU.add).then_inc(taken(p), 1)
                    wait_taken(dve, p)
                    link(V.tensor_tensor(idf[:, :], idf[:, :], idz[:, :], ALU.add))
                    V.tensor_copy(idx[:, 0, :], idf[:, :]).then_inc(s_idx, 1)
                    V.tensor_scalar(idx[:, 1, :], idf[:, :], pad[:, 1:2], None, ALU.add).then_inc(s_idx, 1)
                if name == "ST":
                    wait_product(dve, p)
                    if b == 0:
                        dve.wait_ge(d_c1, 16 * 6)
                    V.tensor_tensor(cand[:, C:C + P], bank(p)[:, 0:P], keys[:, b, :], ALU.mult).then_inc(taken(p), 1)
                    wait_taken(dve, p)
                    if b > 0:
                        dve.wait_ge(s_best, b)
                    best_keys(cand[:, :], best, C, link)
                    V.tensor_copy(cand[:, 0:C], best[:, :]).then_inc(s_best, 1)

            stats(0, 0)
            apply(0, 0)
            def first_queries(c):
                dve.wait_ge(taken((f"Q{c}", 0)), PLACE[f"Q{c}", 0] // 2 + 1)
                link(V.tensor_tensor(qb[:, c, :], qb[:, c, :], sin_s[:, :], ALU.mult))
                V.tensor_tensor(qa[:, c, :], qa[:, c, :], qb[:, c, :], ALU.add).then_inc(s_roped[c], 1)
                dve.wait_ge(s_roped[c], 1)
                dve.wait_ge(s_hi[c], 1)
                V.tensor_tensor(qa[:, c, :], qa[:, c, :], part[:, 0, c, :], ALU.subtract).then_inc(s_res[c], 1)
                dve.wait_ge(s_res[c], 1)
                dve.wait_ge(s_mid[c], 1)
                V.tensor_tensor(part[:, 2, c, :], qa[:, c, :], part[:, 1, c, :], ALU.subtract).then_inc(s_lo[c], 1)

            for name in PROLOGUE:
                consume((name, 0))
            first_queries(0)
            first_queries(1)
            for t in range(END + 1):
                if t < UNITS:
                    s, u = t // 16, t % 16
                    dve.wait_ge(s_p1, t + 1)
                    if u == 0 and s >= 2:
                        wait_product(dve, ("MT", s - 2))
                    V.tensor_reduce(mx[:, s % 2, u:u + 1], score[t % 2][:, 0, :], AX.X, ALU.max).then_inc(s_max, 1)
                for kind, bb in norms_at(t):
                    stats(kind, bb)
                for kind, bb in norms_at(t - 2):
                    apply(kind, bb)
                for p in products_at(t - 1):
                    consume(p)
                for p in products_at(t - 10):
                    if p[0] == "GT":
                        choose(p[1])
                if t == FREE_EARLY:
                    for c in range(3):
                        dve.wait_ge(s_lo[c], NB)
                    dve.wait_ge(d_part[(NB - 1) % 2], 16 * 9 * (NB // 2))
                    for n in range(NOWN, NOWN + NEARLY):
                        ins = V.memset(ew[n][:, EWG + H:EWG + EWD], 0.0)
                    ins.then_inc(s_pad0, 1)
                if t == FREE_ALL:
                    dve.wait_ge(s_av, UNITS // 4)
                    for n in range(NOWN + NEARLY, NOWN + NEARLY + NRING):
                        V.memset(ew[n][:, EWG + H:EWG + EWD], 0.0)
                    V.memset(eat[:, :, 1, :], 0.0).then_inc(s_pad1, 1)
                if ("ST", NB - 1) in products_at(t - 3):
                    dve.wait_ge(d_merge, 16 * NT)
                    best_keys(merged[:, :], best2, C, lambda ins: ins.then_inc(s_tk, 1))
            def slot_weight(j):
                dve.wait_ge(d_gather[j], 16)
                V.tensor_tensor_reduce(out=wtmp[:, j, :], in0=xg[:, j, H:XW], in1=emask[:, j, :], scale=1.0,
                                       scalar=0.0, op0=ALU.mult, op1=ALU.add,
                                       accum_out=wslot[:, j:j + 1]).then_inc(s_ws, 1)
            for j in range(-1, PAIRS):
                n = j + 1
                if n < PAIRS:
                    slot_weight(n)
                if n < PAIRS:
                    dve.wait_ge(e_th, n + 1)
                    if n >= 2:
                        dve.wait_ge(e_at, n - 1)
                    a = egu[:, 2 + n % 2, :]
                    link(V.scalar_tensor_tensor(out=a, in0=egu[:, n % 2, :], scalar=1.0, in1=ps_s[:, n % 2, 0:I],
                                                op0=ALU.add, op1=ALU.mult))
                    V.scalar_tensor_tensor(out=a, in0=a, scalar=0.5, in1=ps_s[:, n % 2, I:2 * I],
                                           op0=ALU.mult, op1=ALU.mult).then_inc(e_act, 1)
                if j >= 0:
                    dve.wait_ge(e_at, j + 1)
                    if j >= 2:
                        dve.wait_ge(e_dn, j - 1)
                    V.tensor_copy(eat[:, j % 2, 0, :], ps_o[:, 0, 0:P])
                    V.tensor_copy(eat[0:I - P, j % 2, 1, :], ps_o[0:I - P, 0, P:2 * P]).then_inc(e_atc, 1)
            for n in range(NB * 2):
                q = n % 4
                dve.wait_ge(d_fin[q], 32 * (n // 4 + 1))
                link(V.tensor_tensor(xs[:, 2 * n:2 * n + 2, :], xs[:, 2 * n:2 * n + 2, :], fin[:, q, 0, :, :], ALU.add))
                V.tensor_tensor(xs[:, 2 * n:2 * n + 2, :], xs[:, 2 * n:2 * n + 2, :], fin[:, q, 1, :, :],
                                ALU.add).then_inc(s_fin, 1)


def kernel(**inputs):
    import numpy as np
    import concourse.bacc as bacc
    from concourse.bass_utils import run_bass_kernel_spmd as run

    f = np.float32
    a = {k[3:]: np.ascontiguousarray(v) for k, v in inputs.items()}
    inv = (f(1.0) / f(10000.0) ** (np.arange(0, HD, 2, dtype=f) / f(HD))).astype(f)
    ang = np.arange(S, dtype=f)[None, :] * np.concatenate([inv, inv])[:, None]
    sign = np.where(np.arange(HD) < HD // 2, -1, 1).astype(f)[:, None]
    p, j = np.arange(P), np.arange(PAIRS)
    tile, lane = np.arange(P)[:, None, None] // E, np.arange(P)[None, None, :]
    token = S * np.arange(NB)[None, :, None] + P * tile + lane
    arrays = {
        "x": a["attn_x"].reshape(T, H),
        "wq": np.ascontiguousarray(a["attn_Wq"].T),
        "wkv": np.ascontiguousarray(np.concatenate([a["attn_Wk"], a["attn_Wv"]]).T),
        "wo": np.ascontiguousarray(a["attn_Wo"].T),
        "gate": np.ascontiguousarray(a["ffn_gate_w"].T),
        "wsgu": a["ffn_ws_gate_up"], "wsd": a["ffn_ws_down"],
        "wgu": a["ffn_w_gate_up"], "wd": a["ffn_w_down"],
        "cosr": np.tile(np.cos(ang), (P // HD, 1)).astype(f),
        "sinr": np.tile(np.sin(ang) * sign, (P // HD, 1)).astype(f),
        "ident_in": np.eye(P, dtype=f),
        "keys_in": (T - token).astype(f),
        "tri_in": np.ascontiguousarray(np.broadcast_to(np.tri(G, k=-1, dtype=f), (P, G, G))),
        "emask_in": (np.arange(E)[None, None, :] == (2 * j[None, :] + (p >= 64)[:, None])[:, :, None]).astype(f),
        "pad_in": np.stack([p, ROWS * (p >= 64)], 1).astype(f),
    }
    nc = bacc.Bacc("TRN2", target_bir_lowering=False, num_devices=1)
    args = [nc.dram_tensor(f"in_{k}", v.shape, mybir.dt.from_np(v.dtype), kind="ExternalInput").ap()
            for k, v in arrays.items()]
    out = nc.dram_tensor("out_0", (T, H), F32, kind="ExternalOutput").ap()
    moe_kernel(nc, *args, out)
    r = run(nc, [{f"in_{k}": v for k, v in arrays.items()}], core_ids=[0])
    return r.results[0]["out_0"].reshape(NB, S, H)
```

```python
from contextlib import ExitStack

import concourse.bass as bass
from concourse import mybir

F32 = mybir.dt.float32
BF16 = mybir.dt.bfloat16
U32 = mybir.dt.uint32
ALU = mybir.AluOpType
ACT = mybir.ActivationFunctionType
AX = mybir.AxisListType

P = 128
NB, S, H = 4, 512, 256
T = NB * S
NT = S // P
HK = H // P
NH, NKV = 16, 4
HD = H // NH
REP = NH // NKV
E, I, TOPK, C = 32, 176, 6, 48
G, TG = 8, 3
EG = E // G
ISH = 2 * I
SCALE_W = 16.0
EPS = 1e-5
ATT_SCALE = float(HD) ** -0.5
PAIRS = E // 2
SIDE = (1, 3, 5, 7, 9, 11)
CHAINS = [[j for j in range(PAIRS) if j not in SIDE], list(SIDE)]
CH = NB * NT // 2
SIDE_POOL = 4
MAIN = [(SIDE_POOL + n) % CH for n in range(CH)]
PACE = (10, 12, 12, 13, 13, 14, 14)
NY = 4
AHEAD = 8
NXG = AHEAD + 2
ROWS = T + P
XW = H + E
MROW = 96
KR = 99
BLOCKS = ((0, 3), (3, 2), (5, 1))

STEPS = NB * NKV
UNITS = STEPS * 16
LAG = 26
AVLAG = LAG + 5
NP = 3
NA, NS = 3, 2
END = UNITS + 80

PRE = [(16, "T0", 1), (17, "T1", 1), (19, "Q0", 2), (22, "Q1", 2), (25, "KV", 2), (28, "VT", 1)]
POST = [(32, "OT0", 1), (33, "OT1", 1), (35, "W0", 2), (37, "W1", 2), (49, "U0", 1), (51, "U1", 1),
        (53, "GL", 1), (54, "A0", 2), (56, "A1", 2), (58, "A2", 2), (60, "A3", 2), (63, "A4", 2),
        (68, "A5", 2), (70, "GT", 1), (72, "D0", 3), (75, "D1", 3), (81, "ST", 1)]
ST_LATE = 108
LAST = [(32, "OT0", 1), (33, "OT1", 1), (35, "W0", 1), (38, "W1", 1), (49, "U0", 1), (51, "U1", 1),
        (53, "GL", 1), (55, "GT", 1), (56, "A0", 2), (58, "A1", 2), (61, "A2", 2), (63, "A3", 2),
        (66, "ST", 1), (67, "A4", 2), (69, "A5", 2), (72, "D0", 1), (73, "KP", 1), (74, "D1", 1)]
WARM = 25
PROLOGUE = ["T0", "T1", "KV", "Q0", "Q1", "VT"]
PARTED, STACKED = (3, 9, 3 + 9, 9 + 9), (6, 9, 6 + 9, 9 + 9)
STACK_OUT, STACK_IN = 39, (44, 54)
FREE_EARLY = 64 * (NB - 2) + 48
FREE_ALL = UNITS + AVLAG + 2
FREE_MID = UNITS + 41
NORM1, NORM2 = 3, 37
NSTATS, NAGGR, NAPPLY = (1, 2, 3, 4), 5, 9


def table():
    out = [(16 * (s + 1) + 2, "MT", s, 1) for s in range(STEPS)]
    out += [(16 * s + AVLAG + 15, "NT", s, 1) for s in range(STEPS)]
    out += [(64 * (b - 1) + u, n, b, w) for b in range(1, NB) for u, n, w in PRE]
    out += [(64 * (b + 1) + (ST_LATE if n == "ST" and b < NB - 2 else u), n, b, w)
            for b in range(NB - 1) for u, n, w in POST]
    out += [(64 * NB + u, n, NB - 1, w) for u, n, w in LAST]
    return sorted(out)


TABLE = table()
for (t0, n0, _, w0), (t1, n1, _, _) in zip(TABLE, TABLE[1:]):
    assert t0 + w0 <= t1, (t0, n0, w0, t1, n1)
ORDER = [(n, 0) for n in PROLOGUE] + [(n, b) for _, n, b, _ in TABLE]
PLACE = {p: n for n, p in enumerate(ORDER)}


def parts_at(t):
    return [((n, b), t - u, w) for u, n, b, w in TABLE if u <= t < u + w]


def products_at(t):
    return [(n, b) for u, n, b, w in TABLE if u + w - 1 == t]


def norms_at(t):
    out = [(0, t // 64 + 1)] if t % 64 == NORM1 and 0 <= t and t // 64 + 1 < NB else []
    return out + ([(1, t // 64 - 1)] if t % 64 == NORM2 and t >= 64 and t // 64 - 1 < NB else [])


NORMS = [(0, 0)] + [n for t in range(END) for n in norms_at(t)]
NORM_AT = {n: i + 1 for i, n in enumerate(NORMS)}


def moe_kernel(nc, x, wq, wkv, wo, gate, wsgu, wsd, wgu, wd, cosr, sinr, ident_in, keys_in, tri_in,
               emask_in, pad_in, out):
    x_scr = nc.dram_tensor("x_scr", [ROWS, XW], F32).ap()
    plane = nc.dram_tensor("plane", [4 * ROWS, H], F32).ap()
    q_scr = nc.dram_tensor("q_scr", [2, 3, HD, NH, S], BF16).ap()
    k_scr = nc.dram_tensor("k_scr", [2, 3, HD, NKV, S], BF16).ap()

    with ExitStack() as ctx:
        def sb(name, shape, dt=F32):
            return ctx.enter_context(nc.sbuf_tensor(name, shape, dt))

        def sem(name):
            return ctx.enter_context(nc.semaphore(name))

        ps_a = ctx.enter_context(nc.psum_tensor("ps_a", [P, 1, S], F32))
        ps_a2 = ctx.enter_context(nc.psum_tensor("ps_a2", [P, 1, S], F32))
        ps_a3 = ctx.enter_context(nc.psum_tensor("ps_a3", [P, 1, S], F32))
        ps_s = ctx.enter_context(nc.psum_tensor("ps_s", [P, NS, S], F32))
        ps_o = ctx.enter_context(nc.psum_tensor("ps_o", [P, 1, S], F32))
        ps_m = ctx.enter_context(nc.psum_tensor("ps_m", [P, 2, S], F32))
        score = [ps_a, ps_a2, ps_a3]

        xs = sb("xs", [P, NB * NT, H])
        tab = sb("tab", [P, 2 * S + HK * H + HK * P])
        cos_s, sin_s = tab[:, 0:S], tab[:, S:2 * S]
        wq_s = tab[:, 2 * S:2 * S + HK * H].rearrange("p (k o) -> p k o", k=HK)
        wkv_s = tab[:, 2 * S + HK * H:].rearrange("p (k o) -> p k o", k=HK)
        wo_s, gate_s = sb("wo_s", [P, HK, H]), sb("gate_s", [P, HK, E])
        wsgu_s, wsd_s = sb("wsgu_s", [P, HK, 2 * ISH]), sb("wsd_s", [P, 3, H])
        ident, keys = sb("ident", [P, P]), sb("keys", [P, NB, P])
        tri, emask, pad = sb("tri", [P, G, G]), sb("emask", [P, PAIRS, E]), sb("pad", [P, 1 + PAIRS])
        early = sb("early", [P, 2 * NT * H + 6 * S + 9 * S // 2])
        xn = early[:, 0:NT * H].rearrange("p (i h) -> p i h", i=NT)
        xt = early[:, NT * H:2 * NT * H].rearrange("p (k s) -> p k s", k=HK)
        qa = early[:, 2 * NT * H:2 * NT * H + 3 * S].rearrange("p (c s) -> p c s", c=3)
        qb = early[:, 2 * NT * H + 3 * S:2 * NT * H + 6 * S].rearrange("p (c s) -> p c s", c=3)
        part = early[:, 2 * NT * H + 6 * S:].bitcast(BF16).rearrange("p (j c s) -> p j c s", j=3, c=3)
        late = sb("late", [P, NT * XW + HK * S + 4 * S])
        xr = late[:, 0:NT * XW].rearrange("p (i w) -> p i w", i=NT)
        xrt = late[:, NT * XW:NT * XW + HK * S].rearrange("p (k s) -> p k s", k=HK)
        hs = late[:, NT * XW + HK * S:NT * XW + HK * S + 3 * S].rearrange("p (c s) -> p c s", c=3)
        th = late[:, NT * XW + HK * S + 3 * S:]
        mid = sb("mid", [P, 2 * S + 2 * NT * NKV * 2 * HD + NT * H + HK * S])
        vt, osb = mid[:, 0:S], mid[:, S:2 * S]
        VSZ = 2 * NT * NKV * 2 * HD
        vs = mid[:, 2 * S:2 * S + VSZ].rearrange("p (b i g d) -> p b i g d", b=2, i=NT, g=NKV)
        od = mid[:, 2 * S + VSZ:2 * S + VSZ + NT * H].rearrange("p (i h) -> p i h", i=NT)
        ot = mid[:, 2 * S + VSZ + NT * H:].rearrange("p (k s) -> p k s", k=HK)
        rec = sb("rec", [P, NT, REP])
        mx, mr, mrow = sb("mx", [P, 2, 16]), sb("mr", [16, P]), sb("mrow", [16, 2, 3, P], BF16)
        stat, agg = sb("stat", [P, 2, NT, 6]), sb("agg", [P, 2, NT, 2])
        rstd, halfs = sb("rstd", [P, 2, NT]), sb("halfs", [P, NT])
        shift = sb("shift", [P, 2, NT])
        lgt, lg = sb("lgt", [P, P]), sb("lg", [P, NT, E])
        gs, cmp, eq = sb("gs", [P, NT, G]), sb("cmp", [P, NT, G, G]), sb("eq", [P, NT, G, G])
        rank, ex, exs = sb("rank", [P, NT, G]), sb("ex", [P, NT, E]), sb("exs", [P, NT, 4])
        top, rep, sel = sb("top", [P, NT, 8]), sb("rep", [P, NT, E]), sb("sel", [P, NT, E])
        cand, best = sb("cand", [P, C + P]), sb("best", [P, C])
        merged, best2 = sb("merged", [E, 4 * C]), sb("best2", [E, 64])
        idf, idz, idx = sb("idf", [P, 16]), sb("idz", [P, 16]), sb("idx", [P, 2, 16], U32)
        wslot, wtmp = sb("wslot", [P, PAIRS]), sb("wtmp", [P, PAIRS, E])
        zero = sb("zero", [P, XW])

        QSB, KSB, PTB = 2 * NH * S // 2, 2 * NKV * S // 2, NP * REP * S
        big = sb("big", [P, QSB + KSB + PTB])
        qs = big[:, 0:QSB].bitcast(BF16).rearrange("p (b h s) -> p b h s", b=2, h=NH)
        ks = big[:, QSB:QSB + KSB].bitcast(BF16).rearrange("p (b h s) -> p b h s", b=2, h=NKV)
        pt = big[:, QSB + KSB:].rearrange("p (n h s) -> p n h s", n=NP, h=REP)
        EWG, EWD = HK * 2 * I, 2 * H
        NOWN = 6
        NEARLY = 5
        NTAB = 1
        NRING = 8
        NMID = 3
        NBUF = NOWN + NEARLY + NTAB + NRING + NMID
        EW = EWG + EWD
        ew = [sb(f"ew{n}", [P, EW]) for n in range(NOWN)]
        ew += [early[:, n * EW:(n + 1) * EW] for n in range(NEARLY)]
        ew += [tab[:, n * EW:(n + 1) * EW] for n in range(NTAB)]
        ew += [big[:, n * EW:(n + 1) * EW] for n in range(NRING)]
        ew += [mid[:, n * EW:(n + 1) * EW] for n in range(NMID)]
        BUF_EARLY = range(NOWN, NOWN + NEARLY + NTAB)
        BUF_BIG = range(NBUF - NRING - NMID, NBUF - NMID)
        BUF_MID = range(NBUF - NMID, NBUF)
        at0 = NRING * EW
        xg = big[:, at0:at0 + NXG * XW].rearrange("p (j w) -> p j w", j=NXG)
        at0 += NXG * XW
        xgt = big[:, at0:at0 + 2 * H].rearrange("p (n k c) -> p n k c", n=2, k=HK)
        at0 += 2 * H
        egu = big[:, at0:at0 + 4 * I].rearrange("p (n f) -> p n f", n=4)
        at0 += 4 * I
        eat = big[:, at0:at0 + 2 * H].rearrange("p (n k c) -> p n k c", n=2, k=2)
        at0 += 2 * H
        ey = big[:, at0:at0 + NY * H].rearrange("p (n o) -> p n o", n=NY)
        at0 += NY * H
        assert E - NBUF <= BUF_BIG[-4]
        FREE = big[:, (NRING - 4) * EW:(NRING - 4) * EW + 16 * H]
        fin = [t[:, 4 * H * n:4 * H * n + 4 * H].rearrange("p (a i o) -> p a i o", a=2, i=2)
               for t in (late, FREE) for n in range(CH // 2)]
        assert at0 <= QSB + KSB + PTB, (at0, QSB + KSB + PTB)

        d_x = [sem(f"d_x{b}") for b in range(NB)]
        d_c0, d_c1 = sem("d_c0"), sem("d_c1")
        d_wqkv, d_wsh = sem("d_wqkv"), sem("d_wsh")
        d_ew = [sem(f"d_ew{n}") for n in range(NBUF)]
        d_part = [sem("d_part0"), sem("d_part1")]
        d_first, d_begin = [sem(f"d_first{n}") for n in range(6)], sem("d_begin")
        d_stack = [sem("d_stack0"), sem("d_stack1")]
        d_mrow = [sem("d_mrow0"), sem("d_mrow1")]
        d_scr, d_zero, d_merge = sem("d_scr"), sem("d_zero"), sem("d_merge")
        d_gather, d_plane = [sem(f"d_gather{j}") for j in range(PAIRS)], [sem("d_plane0"), sem("d_plane1")]
        d_fin, d_out = [sem(f"d_fin{n}") for n in range(CH)], sem("d_out")
        s_zero, s_const, s_ones, s_dve, s_pool = sem("s_zero"), sem("s_const"), sem("s_ones"), sem("s_dve"), sem("s_pool")
        s_p1, s_max = sem("s_p1"), sem("s_max")
        s_p2, s_exp = sem("s_p2"), sem("s_exp")
        s_av, s_out = sem("s_av"), sem("s_out")
        m_full = [sem("m_full0"), sem("m_full1")]
        m_taken = [sem("m_taken0"), sem("m_taken1")]
        s_stat, s_var, s_rstd, s_xn = sem("s_stat"), sem("s_var"), sem("s_rstd"), sem("s_xn")
        s_roped, s_hi, s_res, s_mid, s_lo = ([sem(f"s_{n}{c}") for c in range(3)]
                                             for n in ("roped", "hi", "res", "mid", "lo"))
        s_mrow, s_tanh, s_vt = sem("s_mrow"), sem("s_tanh"), sem("s_vt")
        s_mask, s_ex, s_sel, s_row = sem("s_mask"), sem("s_ex"), sem("s_sel"), sem("s_row")
        s_best, s_tk, s_idx, s_ws = sem("s_best"), sem("s_tk"), sem("s_idx"), sem("s_ws")
        s_pad0, s_pad1, s_pad2, s_fin, s_side = sem("s_pad0"), sem("s_pad1"), sem("s_pad2"), sem("s_fin"), sem("s_side")
        e_xt, e_xtc, e_gu, e_th = sem("e_xt"), sem("e_xtc"), sem("e_gu"), sem("e_th")
        e_act, e_at, e_atc, e_dn, e_y = sem("e_act"), sem("e_at"), sem("e_atc"), sem("e_dn"), sem("e_y")
        RING = [(e % NBUF, e // NBUF) for e in range(E)]

        def bank(p):
            return ps_m[:, PLACE[p] % 2, :]

        def wait_bank(eng, p):
            n = PLACE[p]
            if n >= 2:
                eng.wait_ge(m_taken[n % 2], n // 2)

        def wait_product(eng, p):
            eng.wait_ge(m_full[PLACE[p] % 2], PLACE[p] // 2 + 1)

        def full(p):
            return m_full[PLACE[p] % 2]

        def taken(p):
            return m_taken[PLACE[p] % 2]

        def wait_taken(eng, p):
            eng.wait_ge(m_taken[PLACE[p] % 2], PLACE[p] // 2 + 1)

        def wait_added(eng, j):
            c = int(j in SIDE)
            eng.wait_ge(d_plane[c], 16 * (CHAINS[c].index(j) + 1))

        def wait_side(eng, m):
            if m < SIDE_POOL:
                eng.wait_ge(s_side, m + 1)
            else:
                eng.wait_ge(s_fin, m - SIDE_POOL + 1)

        block = ctx.enter_context(nc.Block())

        @block.sync
        def _(sp):
            for b in range(NB):
                sp.dma_start(xs[:, NT * b:NT * b + NT, :],
                             x[S * b:S * b + S, :].rearrange("(i p) h -> p i h", p=P)).then_inc(d_x[b], 16)
                if b == 0:
                    sp.dma_start(ident[:, :], ident_in).then_inc(d_c0, 16)
                    sp.dma_start(wkv_s[:, :, :], wkv.rearrange("(k p) o -> p k o", p=P)).then_inc(d_wqkv, 16)
                    sp.dma_start(wq_s[:, :, :], wq.rearrange("(k p) o -> p k o", p=P)).then_inc(d_wqkv, 16)
                    sp.dma_start(cos_s[:, :], cosr).then_inc(d_c0, 16)
                    sp.dma_start(sin_s[:, :], sinr).then_inc(d_c0, 16)

            def q_rows(q, j, c):
                return q_scr[q, j, :, 8 * c:8 * c + 8, :].rearrange("d h s -> h d s")

            def k_rows(q, j):
                return k_scr[q, j].rearrange("d h s -> h d s")

            def stack_out(b):
                q = b % 2
                for c in range(3):
                    sp.wait_ge(s_lo[c], b + 1)
                if b >= 2:
                    sp.wait_ge(d_stack[q], 16 * STACKED[b - 2])
                    sp.wait_ge(d_begin, 16 * 9)
                for j in range(3):
                    for m in range(2):
                        sp.dma_start(q_rows(q, j, m), part[:, j, m, :]).then_inc(d_part[q], 16)
                    sp.dma_start(k_rows(q, j), part[0:NKV * HD, j, 2, :]).then_inc(d_part[q], 16)

            def queries_in(q, j, h0, h1, sem):
                r, n = BLOCKS[j]
                for m in range(r, r + n):
                    sp.dma_start(qs[16 * m:16 * m + 16, q, h0:h1, :], q_scr[q, j, :, h0:h1, :]).then_inc(sem, 16)

            def parts_in(q, j, sem):
                r, n = BLOCKS[j]
                sp.dma_start(ks[16 * r:16 * r + 16 * n, q, :, :],
                             k_scr[q, 0:n].rearrange("j d h s -> (j d) h s")).then_inc(sem, 16)

            def stack_in(b, half):
                q = b % 2
                sp.wait_ge(d_part[q], 16 * PARTED[b])
                if b >= 2:
                    sp.wait_ge(s_p2, 64 * (b - 1))
                for j in (0,) if half == 0 else (1, 2):
                    queries_in(q, j, 0, NH, d_stack[q])
                for j in range(3) if half == 0 else ():
                    parts_in(q, j, d_stack[q])

            def weights(e):
                n, turn = RING[e]
                if turn >= 1:
                    sp.wait_ge(e_dn, (e - NBUF) // 2 + 1)
                t = ew[n]
                sp.dma_start(t[:, 0:EWG].rearrange("p (k f) -> p k f", k=HK),
                             wgu[e].rearrange("(k p) f -> p k f", p=P)).then_inc(d_ew[n], 16)
                sp.dma_start(t[:, EWG:EWG + H], wd[e, 0:P, :]).then_inc(d_ew[n], 16)
                sp.dma_start(t[0:I - P, EWG + H:EW], wd[e, P:I, :]).then_inc(d_ew[n], 16)

            def first_out(c, j, ready):
                sp.wait_ge(ready[c], 1)
                dst = k_rows(0, j) if c == 2 else q_rows(0, j, c)
                sp.dma_start(dst, part[0:NKV * HD if c == 2 else P, j, c, :]).then_inc(
                    d_part[0] if c == 1 else d_first[3 * (c == 2) + j], 16)

            def first_in(j):
                sp.wait_ge(d_first[j], 16)
                queries_in(0, j, 0, NH // 2, d_begin)

            first_out(2, 0, s_hi)
            first_out(2, 1, s_mid)
            first_out(0, 0, s_hi)
            first_out(2, 2, s_lo)
            first_out(0, 1, s_mid)
            first_out(0, 2, s_lo)
            first_in(0)
            for j in range(3):
                sp.wait_ge(d_first[3 + j], 16)
            for j in range(3):
                parts_in(0, j, d_begin)
            first_in(1)
            first_in(2)
            first_out(1, 0, s_hi)
            first_out(1, 1, s_mid)
            first_out(1, 2, s_lo)
            sp.wait_ge(d_part[0], 16 * PARTED[0])
            for j in range(3):
                queries_in(0, j, NH // 2, NH, d_stack[0])
            sp.wait_ge(s_const, 1)
            sp.dma_start(wo_s[:, :, :], wo.rearrange("(k p) o -> p k o", p=P)).then_inc(d_c1, 16)
            sp.dma_start(gate_s[:, :, :], gate.rearrange("(k p) o -> p k o", p=P)).then_inc(d_c1, 16)
            sp.dma_start(keys[:, :, :], keys_in).then_inc(d_c1, 16)
            sp.dma_start(tri[:, :, :], tri_in).then_inc(d_c1, 16)
            sp.dma_start(emask[:, :, :], emask_in).then_inc(d_c1, 16)
            sp.dma_start(pad[:, :], pad_in).then_inc(d_c1, 16)
            sp.dma_start(wsgu_s[:, :, :], wsgu.rearrange("(k p) o -> p k o", p=P)).then_inc(d_wsh, 16)
            sp.dma_start(wsd_s[:, 0:2, :], wsd[0:2 * P, :].rearrange("(k p) o -> p k o", p=P)).then_inc(d_wsh, 16)
            sp.dma_start(wsd_s[0:ISH - 2 * P, 2, :], wsd[2 * P:ISH, :]).then_inc(d_wsh, 16)
            sp.dma_start(x_scr[T:ROWS, :], zero[:, :]).then_inc(d_scr, 16)
            for t in range(END + 1):
                for name, b in products_at(t - 1):
                    if name == "MT":
                        g, q = b % NKV, b // NKV % 2
                        sp.wait_ge(s_mrow, b + 1)
                        if b >= 8:
                            sp.wait_ge(s_p2, 16 * (b - 7))
                        for j in range(3):
                            sp.dma_start(qs[MROW + j:MROW + j + 1, q, REP * g:REP * g + REP, :]
                                         .rearrange("o h (i p) -> o (h i) p", p=P),
                                         mrow[0:16, b % 2, j, :]).then_inc(d_mrow[b % 2], 16)
                    if name == "ST":
                        if b == NB - 1:
                            sp.wait_ge(s_best, NB)
                            for i in range(NT):
                                sp.dma_start(merged[:, C * i:C * i + C],
                                             best[E * i:E * i + E, :]).then_inc(d_merge, 16)
                for name, b in products_at(t - 11):
                    if name == "GT":
                        sp.wait_ge(s_row, b + 1)
                        sp.dma_start(x_scr[S * b:S * b + S, :].rearrange("(i p) w -> p i w", p=P),
                                     xr[:, :, :]).then_inc(d_scr, 16)
                if t % 64 == STACK_OUT and t // 64 + 1 < NB:
                    stack_out(t // 64 + 1)
                if t % 64 in STACK_IN and t // 64 + 1 < NB:
                    stack_in(t // 64 + 1, STACK_IN.index(t % 64))
                if t < 16 * NOWN and t % 16 == 8:
                    weights(t // 16)
                if t % 8 == 3 and t // 8 < ROWS // P:
                    n = 4 * (t // 8)
                    sp.dma_start(plane[P * n:P * n + 4 * P, :].rearrange("(i p) h -> p i h", p=P),
                                 zero[:, None, 0:H].broadcast_to([P, 4, H])).then_inc(d_zero, 16)
                if t == FREE_EARLY + 4:
                    sp.wait_ge(s_pad0, 1)
                if (t - FREE_EARLY) % 8 == 4 and 0 <= (t - FREE_EARLY) // 8 < NEARLY + NTAB:
                    weights(BUF_EARLY[(t - FREE_EARLY) // 8])
                if t == FREE_ALL + 2:
                    sp.wait_ge(s_pad1, 1)
                    for e in BUF_BIG:
                        weights(e)
                if t == FREE_MID + 2:
                    sp.wait_ge(s_pad2, 1)
                    for e in BUF_MID:
                        weights(e)
            for e in range(NBUF, E):
                weights(e)
            for c in (1, 0):
                wait_added(sp, CHAINS[c][-1])
                for n in range(CH):
                    m = MAIN[n] if c == 0 else n
                    if c == 0:
                        wait_side(sp, m)
                    elif m > 0 and PACE[m - 1]:
                        wait_added(sp, PACE[m - 1])
                    for half in range(2):
                        row = (2 * c + half) * ROWS + 2 * P * m
                        sp.dma_start(fin[m][:, half, :, :],
                                     plane[row:row + 2 * P, :].rearrange("(i p) h -> p i h", p=P)).then_inc(d_fin[m], 16)
            sp.wait_ge(d_out, 16 * NB * 2)

        @block.tensor
        def _(pe):
            def product(p, part=0, parts=1):
                name, b = p
                first, last = part == 0, part == parts - 1
                if name in ("T0", "T1"):
                    k = int(name[1])
                    if p == ORDER[0]:
                        pe.wait_ge(d_c0, 16 * 3)
                    pe.wait_ge(s_xn, NORM_AT[0, b])
                    wait_bank(pe, p)
                    for i in range(NT):
                        mm = pe.transpose(bank(p)[:, P * i:P * i + P], xn[:, i, P * k:P * k + P], ident[:, :])
                elif name in ("Q0", "Q1", "KV"):
                    if name == ("KV" if b == 0 else "Q0") and first:
                        if b == 0:
                            pe.wait_ge(d_wqkv, 32)
                        wait_taken(pe, ("T0", b))
                        wait_taken(pe, ("T1", b))
                    w = wkv_s[:, :, :] if name == "KV" else wq_s[:, :, P * int(name[1]):P * int(name[1]) + P]
                    if first:
                        wait_bank(pe, p)
                    for k in range(HK)[part::parts]:
                        mm = pe.matmul(bank(p), w[:, k, :], xt[:, k, :], start=(k == 0), stop=(k == HK - 1))
                elif name == "VT":
                    pe.wait_ge(s_vt, b + 1)
                    wait_bank(pe, p)
                    for i in range(NT):
                        mm = pe.transpose(bank(p)[:, 64 * i:64 * i + 64], vt[64:P, P * i:P * i + P],
                                          ident[64:P, 64:P])
                elif name == "MT":
                    pe.wait_ge(s_max, 16 * (b + 1))
                    wait_bank(pe, p)
                    mm = pe.transpose(bank(p)[0:16, 0:P], mx[:, b % 2, :], ident[:, :])
                elif name == "NT":
                    pe.wait_ge(s_out, b + 1)
                    wait_bank(pe, p)
                    for i in range(NT):
                        mm = pe.transpose(bank(p)[:, P * i:P * i + P], osb[:, P * i:P * i + P], ident[:, :])
                elif name in ("OT0", "OT1"):
                    k = int(name[2])
                    wait_taken(pe, ("NT", NKV * b + NKV - 1))
                    wait_bank(pe, p)
                    for i in range(NT):
                        mm = pe.transpose(bank(p)[:, P * i:P * i + P], od[:, i, P * k:P * k + P], ident[:, :])
                elif name in ("W0", "W1"):
                    if name == "W0" and first:
                        wait_taken(pe, ("OT0", b))
                        wait_taken(pe, ("OT1", b))
                        if b == 0:
                            pe.wait_ge(d_c1, 16 * 6)
                    if first:
                        wait_bank(pe, p)
                    for n in range(2)[part::parts]:
                        i = 2 * int(name[1]) + n
                        for k in range(HK):
                            mm = pe.matmul(bank(p)[:, H * n:H * n + H], ot[:, k, P * i:P * i + P], wo_s[:, k, :],
                                           start=(k == 0), stop=(k == HK - 1))
                elif name in ("U0", "U1"):
                    k = int(name[1])
                    pe.wait_ge(s_xn, NORM_AT[1, b] + (b == NB - 1))
                    wait_bank(pe, p)
                    for i in range(NT):
                        mm = pe.transpose(bank(p)[:, P * i:P * i + P], xr[:, i, P * k:P * k + P], ident[:, :])
                elif name == "GL":
                    wait_taken(pe, ("U0", b))
                    wait_taken(pe, ("U1", b))
                    wait_bank(pe, p)
                    for k in range(HK):
                        for i in range(NT):
                            mm = pe.matmul(bank(p)[E * i:E * i + E, 0:P], gate_s[:, k, :], xrt[:, k, P * i:P * i + P],
                                           start=(k == 0), stop=(k == HK - 1), skip_group_check=True)
                elif name == "GT":
                    wait_taken(pe, ("GL", b))
                    wait_bank(pe, p)
                    mm = pe.transpose(bank(p)[:, 0:P], lgt[:, :], ident[:, :])
                elif name == "ST":
                    pe.wait_ge(s_sel, b + 1)
                    wait_bank(pe, p)
                    mm = pe.transpose(bank(p)[:, 0:P], sel[:, :, :], ident[:, :])
                elif name == "KP":
                    pe.wait_ge(s_tk, 1)
                    wait_bank(pe, p)
                    for half in range(2):
                        mm = pe.matmul(bank(p)[64 * half:64 * half + 64, 0:PAIRS], best2[:, :],
                                       ident[0:E, half:E:2], start=True, stop=True, skip_group_check=True)
                elif name[0] == "A":
                    c, up = int(name[1]) // 2, int(name[1]) % 2
                    m = min(P, ISH - P * c)
                    if p == ("A0", 0) and first:
                        pe.wait_ge(d_wsh, 16 * 3)
                    if first:
                        wait_bank(pe, p)
                    for k in range(HK)[part::parts]:
                        mm = pe.matmul(bank(p)[0:m, :], wsgu_s[:, k, ISH * up + P * c:ISH * up + P * c + m],
                                       xrt[:, k, :], start=(k == 0), stop=(k == HK - 1))
                else:
                    if first:
                        wait_taken(pe, ("A5", b))
                        wait_bank(pe, p)
                    for m in range(6)[6 // parts * part:6 // parts * (part + 1)]:
                        n, c = m // 3, m % 3
                        i = 2 * int(name[1]) + n
                        mm = pe.matmul(bank(p)[:, H * n:H * n + H], hs[:, c, P * i:P * i + P], wsd_s[:, c, :],
                                       start=(c == 0), stop=(c == 2))
                if last:
                    mm.then_inc(full(p), 1)

            def keep_clock(n):
                zeros = zero[:, :].bitcast(BF16)
                for _ in range(n):
                    pe.matmul(ps_a3[:, 0, :], zeros[:, 0:P], zeros[:, 0:S], start=True, stop=True)

            pe.wait_ge(s_zero, 1)
            keep_clock(WARM)
            for name in PROLOGUE:
                product((name, 0))
            for t in range(END):
                if t < UNITS:
                    s, hl, i = t // 16, t // 4 % 4, t % 4
                    b, g = s // NKV, s % NKV
                    if t == 0:
                        pe.wait_ge(d_begin, 16 * 9)
                    if t == 32:
                        pe.wait_ge(d_stack[0], 16 * STACKED[0])
                    if t % 64 == 0 and t > 0:
                        pe.wait_ge(d_stack[b % 2], 16 * STACKED[b])
                    if t >= NA:
                        pe.wait_ge(s_max, t - NA + 1)
                    pe.matmul(score[t % NA][:, 0, :], qs[0:MROW, b % 2, REP * g + hl, P * i:P * i + P],
                              ks[0:MROW, b % 2, g, :], start=True, stop=True).then_inc(s_p1, 1)
                v = t - LAG
                if 0 <= v < UNITS:
                    s, kt, hl = v // 16, v // 4 % 4, v % 4
                    b, g = s // NKV, s % NKV
                    if v == 0:
                        pe.wait_ge(s_ones, 1)
                    if v % 16 == 0:
                        pe.wait_ge(d_mrow[s % 2], 16 * 3 * (s // 2 + 1))
                    if v >= NS:
                        pe.wait_ge(s_exp, v - NS + 1)
                    pe.matmul(ps_s[:, v % NS, :], ks[0:KR, b % 2, g, P * kt:P * kt + P],
                              qs[0:KR, b % 2, REP * g + hl, :], start=True, stop=True).then_inc(s_p2, 1)
                if 0 <= t - AVLAG < UNITS and (t - AVLAG) % 4 == 0:
                    n = (t - AVLAG) // 4
                    s, kt = n // 4, n % 4
                    pe.wait_ge(s_exp, 4 * n + 4)
                    if kt == 0 and s >= 1:
                        pe.wait_ge(s_out, s)
                    if kt == 0 and s % NKV == 0:
                        wait_taken(pe, ("VT", s // NKV))
                    for hl in range(REP):
                        mm = pe.matmul(ps_o[32 * hl:32 * hl + 32, 0, :], vs[:, s // NKV % 2, kt, s % NKV, :],
                                       pt[:, n % NP, hl, :], start=(kt == 0), stop=(kt == 3), skip_group_check=True)
                    mm.then_inc(s_av, 1)
                for p, n, parts in parts_at(t):
                    product(p, n, parts)

            def x_turn(j):
                pe.wait_ge(d_gather[j], 16)
                if j >= 2:
                    pe.wait_ge(e_xtc, j - 1)
                for k in range(HK):
                    mm = pe.transpose(score[j % 2][:, 0, P * k:P * k + P], xg[:, j % NXG, P * k:P * k + P], ident[:, :])
                mm.then_inc(e_xt, 1)

            def gate_up(j):
                pe.wait_ge(e_xtc, j + 1)
                if j >= 2:
                    pe.wait_ge(e_act, j - 1)
                for half in range(2):
                    slot, turn = RING[2 * j + half]
                    pe.wait_ge(d_ew[slot], 48 * (turn + 1))
                for k in range(HK):
                    for half in range(2):
                        w = ew[RING[2 * j + half][0]]
                        mm = pe.matmul(ps_s[64 * half:64 * half + 64, j % 2, 0:2 * I],
                                       xgt[:, j % 2, k, 64 * half:64 * half + 64],
                                       w[:, 2 * I * k:2 * I * k + 2 * I],
                                       start=(k == 0), stop=(k == HK - 1), skip_group_check=True)
                mm.then_inc(e_gu, 1)

            def act_turn(j):
                pe.wait_ge(e_act, j + 1)
                if j >= 1:
                    pe.wait_ge(e_atc, j)
                pe.transpose(ps_o[:, 0, 0:P], egu[:, 2 + j % 2, 0:P], ident[:, :])
                pe.transpose(ps_o[0:I - P, 0, P:2 * P], egu[:, 2 + j % 2, P:I], ident[:, :]).then_inc(e_at, 1)

            def down(j):
                pe.wait_ge(e_atc, j + 1)
                if j >= 2:
                    pe.wait_ge(e_y, j - 1)
                for k in range(2):
                    for half in range(2):
                        w = ew[RING[2 * j + half][0]]
                        mm = pe.matmul(ps_m[64 * half:64 * half + 64, j % 2, 0:H],
                                       eat[:, j % 2, k, 64 * half:64 * half + 64],
                                       w[:, EWG + H * k:EWG + H * k + H],
                                       start=(k == 0), stop=(k == 1), skip_group_check=True)
                mm.then_inc(e_dn, 1)

            for n in range(len(ORDER) - 2, len(ORDER)):
                wait_taken(pe, ORDER[n])
            for j in range(-2, PAIRS):
                if j + 2 < PAIRS:
                    x_turn(j + 2)
                if j >= 0:
                    act_turn(j)
                if 0 <= j + 1 < PAIRS:
                    gate_up(j + 1)
                if j >= 0:
                    down(j)

        @block.scalar
        def _(act):
            def consume(p):
                name, b = p
                if name in ("T0", "T1", "U0", "U1"):
                    dst = (xt if name[0] == "T" else xrt)[:, int(name[1]), :]
                    wait_product(act, p)
                    if name == "T0" and b > 0:
                        wait_product(act, ("KV", b - 1))
                    if name == "U0" and b > 0:
                        wait_product(act, ("A5", b - 1))
                    nc.scalar.activation(dst, bank(p), ACT.Copy).then_inc(taken(p), 1)
                if name in ("OT0", "OT1"):
                    wait_product(act, p)
                    if name == "OT0" and b > 0:
                        wait_product(act, ("W1", b - 1))
                    nc.scalar.activation(ot[:, int(name[2]), :], bank(p), ACT.Copy).then_inc(taken(p), 1)
                if name == "KV":
                    wait_product(act, p)
                    if b > 0:
                        wait_product(act, ("VT", b - 1))
                    nc.scalar.activation(vt[64:P, :], bank(p)[64:P, :], ACT.Copy).then_inc(s_vt, 1)
                if name == "VT":
                    wait_product(act, p)
                    if b >= 2:
                        act.wait_ge(s_av, 16 * (b - 1))
                    nc.scalar.activation(vs[:, b % 2, :, :, 0:HD],
                                         bank(p)[:, 0:NT * NKV * HD].rearrange("p (i g d) -> p i g d", i=NT, g=NKV),
                                         ACT.Copy).then_inc(taken(p), 1)
                if name == "GL":
                    wait_product(act, p)
                    nc.scalar.activation(lgt[:, :], bank(p)[:, 0:P], ACT.Copy).then_inc(taken(p), 1)
                if name in ("A0", "A2", "A4"):
                    c = int(name[1]) // 2
                    m = min(P, ISH - P * c)
                    wait_product(act, p)
                    if (c, b) != (0, 0):
                        wait_taken(act, (f"A{2 * c - 2}", b) if c else ("A4", b - 1))
                    nc.scalar.activation(th[0:m, :], bank(p)[0:m, :], ACT.Tanh, scale=0.5).then_inc(s_tanh, 1)

            def apply(kind, b, half):
                if half == 0:
                    act.wait_ge(s_rstd, NORM_AT[kind, b])
                    if kind == 0 and b > 0:
                        wait_product(act, ("T1", b - 1))
                        wait_product(act, ("T0", b - 1))
                    if kind == 1 and b > 0:
                        act.wait_ge(d_scr, 16 * (b + 1))
                if (kind, b, half) == (1, NB - 1, 1):
                    return
                for i in (2 * half, 2 * half + 1):
                    ins = nc.scalar.activation(xn[:, i, :] if kind == 0 else xr[:, i, 0:H], xs[:, NT * b + i, :],
                                               ACT.Identity, bias=shift[:, kind, i:i + 1],
                                               scale=rstd[:, kind, i:i + 1])
                if half == 1 or (kind, b) == (1, NB - 1):
                    ins.then_inc(s_xn, 1)

            def gate_exp(b):
                act.wait_ge(s_mask, b + 1)
                nc.scalar.activation(ex[:, :, :], lg[:, :, :], ACT.Exp).then_inc(s_ex, 1)

            def high(p):
                c = ("Q0", "Q1", "KV").index(p[0])
                m = P if c < 2 else NKV * HD
                act.wait_ge(s_roped[c], p[1] + 1)
                if p[1] > 0:
                    act.wait_ge(d_part[(p[1] - 1) % 2], 16 * PARTED[p[1] - 1])
                    act.wait_ge(d_begin, 16 * 9)
                nc.scalar.activation(part[0:m, 0, c, :], qa[0:m, c, :], ACT.Copy).then_inc(s_hi[c], 1)

            def middle(p):
                c = ("Q0", "Q1", "KV").index(p[0])
                m = P if c < 2 else NKV * HD
                act.wait_ge(s_res[c], p[1] + 1)
                nc.scalar.activation(part[0:m, 1, c, :], qa[0:m, c, :], ACT.Copy).then_inc(s_mid[c], 1)

            apply(0, 0, 0)
            apply(0, 0, 1)
            consume(("T0", 0))
            consume(("T1", 0))
            consume(("KV", 0))
            high(("KV", 0))
            middle(("KV", 0))
            high(("Q0", 0))
            middle(("Q0", 0))
            consume(("VT", 0))
            high(("Q1", 0))
            middle(("Q1", 0))
            for t in range(END + 1):
                v = t - LAG
                if 0 <= v < UNITS:
                    n, hl = v // 4, v % 4
                    act.wait_ge(s_p2, v + 1)
                    if n >= NP and hl == 0:
                        act.wait_ge(s_av, n - NP + 1)
                    nc.scalar.activation(pt[:, n % NP, hl, :], ps_s[:, v % NS, :], ACT.Exp,
                                         scale=ATT_SCALE).then_inc(s_exp, 1)
                for p in products_at(t - 1):
                    consume(p)
                for p in products_at(t - 5):
                    if p[0] in ("Q0", "Q1", "KV"):
                        high(p)
                for p in products_at(t - 10):
                    if p[0] in ("Q0", "Q1", "KV"):
                        middle(p)
                for h in range(2):
                    for kind, b in norms_at(t - NAPPLY - h):
                        apply(kind, b, h)
                for p in products_at(t - 5):
                    if p[0] == "GT":
                        gate_exp(p[1])
                if (t - AVLAG - 13) % 16 == 0 and 0 <= (t - AVLAG - 13) // 16 < STEPS:
                    s = (t - AVLAG - 13) // 16
                    act.wait_ge(s_av, 4 * s + 4)
                    if s >= 1:
                        wait_product(act, ("NT", s - 1))
                    nc.scalar.activation(osb[:, :], ps_o[:, 0, :], ACT.Copy).then_inc(s_out, 1)
            for j in range(-2, PAIRS):
                if j + 2 < PAIRS:
                    n = j + 2
                    act.wait_ge(e_xt, n + 1)
                    if n >= 2:
                        act.wait_ge(e_gu, n - 1)
                    nc.scalar.activation(xgt[:, n % 2, :, :], score[n % 2][:, 0, 0:H].rearrange("p (k c) -> p k c", k=HK),
                                         ACT.Copy).then_inc(e_xtc, 1)
                if 0 <= j + 1 < PAIRS:
                    n = j + 1
                    act.wait_ge(e_gu, n + 1)
                    if n >= 2:
                        act.wait_ge(e_act, n - 1)
                    nc.scalar.activation(egu[:, n % 2, :], ps_s[:, n % 2, 0:I], ACT.Tanh, scale=0.5).then_inc(e_th, 1)
                if j >= 0:
                    act.wait_ge(e_dn, j + 1)
                    act.wait_ge(s_ws, j + 1)
                    if j >= NY:
                        wait_added(act, j - NY)
                    nc.scalar.activation(ey[:, j % NY, :], ps_m[:, j % 2, 0:H], ACT.Copy,
                                         scale=wslot[:, j:j + 1]).then_inc(e_y, 1)
            for n, m in enumerate(MAIN):
                act.wait_ge(s_fin, CH - SIDE_POOL + n + 1)
                act.dma_start(out[2 * P * m:2 * P * m + 2 * P, :].rearrange("(i p) h -> p i h", p=P),
                              xs[:, 2 * m:2 * m + 2, :]).then_inc(d_out, 16)

        @block.gpsimd
        def _(pool):
            count = [0]

            def link(ins):
                count[0] += 1
                ins.then_inc(s_pool, 1)
                pool.wait_ge(s_pool, count[0])

            def rope(p):
                name, b = p
                c = ("Q0", "Q1", "KV").index(name)
                m = P if c < 2 else NKV * HD
                wait_taken(pool, p)
                g = nc.gpsimd
                link(g.tensor_tensor(qb[0:m, c, :], qb[0:m, c, :], sin_s[0:m, :], ALU.mult))
                g.tensor_tensor(qa[0:m, c, :], qa[0:m, c, :], qb[0:m, c, :], ALU.add).then_inc(s_roped[c], 1)

            def rest(p):
                c = ("Q0", "Q1", "KV").index(p[0])
                m = P if c < 2 else NKV * HD
                pool.wait_ge(s_roped[c], p[1] + 1)
                pool.wait_ge(s_hi[c], p[1] + 1)
                nc.gpsimd.tensor_tensor(qa[0:m, c, :], qa[0:m, c, :], part[0:m, 0, c, :],
                                        ALU.subtract).then_inc(s_res[c], 1)

            def low(p):
                c = ("Q0", "Q1", "KV").index(p[0])
                m = P if c < 2 else NKV * HD
                pool.wait_ge(s_res[c], p[1] + 1)
                pool.wait_ge(s_mid[c], p[1] + 1)
                nc.gpsimd.tensor_tensor(part[0:m, 2, c, :], qa[0:m, c, :], part[0:m, 1, c, :],
                                        ALU.subtract).then_inc(s_lo[c], 1)

            def root(n, which):
                pool.wait_ge(s_var, n)
                link(nc.gpsimd.tensor_tensor(rstd[:, which, :], rstd[:, which, :], halfs[:, :], ALU.pow))
                nc.gpsimd.tensor_tensor(shift[:, which, :], shift[:, which, :], rstd[:, which, :],
                                        ALU.mult).then_inc(s_rstd, 1)

            root(1, 0)
            pool.wait_ge(s_rstd, 1)
            link(nc.gpsimd.memset(ks[MROW:P, :, :, :], 1.0))
            nc.gpsimd.memset(vs[:, :, :, :, HD:2 * HD], 1.0).then_inc(s_ones, 1)
            pool.wait_ge(s_ones, 1)
            rope(("Q1", 0))
            rest(("Q1", 0))
            low(("Q1", 0))
            for t in range(END + 1):
                for kind, bb in norms_at(t - NAGGR):
                    root(NORM_AT[kind, bb], kind)
                if t == FREE_EARLY:
                    for c in range(3):
                        pool.wait_ge(s_lo[c], NB)
                    pool.wait_ge(d_part[(NB - 1) % 2], 16 * PARTED[NB - 1])
                    for n in BUF_EARLY:
                        ins = nc.gpsimd.memset(ew[n][:, EWG + H:EW], 0.0)
                    ins.then_inc(s_pad0, 1)
                if t == FREE_ALL:
                    pool.wait_ge(s_av, UNITS // 4)
                    for n in BUF_BIG:
                        nc.gpsimd.memset(ew[n][:, EWG + H:EW], 0.0)
                    nc.gpsimd.memset(eat[:, :, 1, :], 0.0).then_inc(s_pad1, 1)
                if t == FREE_MID:
                    wait_product(pool, ("W1", NB - 1))
                    for n in BUF_MID:
                        ins = nc.gpsimd.memset(ew[n][:, EWG + H:EW], 0.0)
                    ins.then_inc(s_pad2, 1)
                for delay, piece in ((1, rope), (6, rest), (11, low)):
                    for p in products_at(t - delay):
                        if p[0] in ("Q0", "Q1", "KV"):
                            piece(p)
            pool.wait_ge(s_idx, 2)
            pool.wait_ge(d_scr, 16 * (NB + 1))
            pool.wait_ge(s_pad1, 1)
            for j in range(-AHEAD, PAIRS):
                if j + AHEAD < PAIRS:
                    n = j + AHEAD
                    if n >= NXG:
                        pool.wait_ge(e_xt, n - NXG + 1)
                        pool.wait_ge(s_ws, n - NXG + 1)
                    nc.gpsimd.indirect_dma_start(out=xg[:, n % NXG, :], out_offset=None, in_=x_scr,
                                                 in_offset=bass.IndirectOffsetOnAxis(ap=idx[:, 0, n:n + 1], axis=0),
                                                 ).then_inc(d_gather[n], 16)
                if j == 0:
                    pool.wait_ge(d_zero, 16 * (ROWS // P))
                if j >= 0:
                    c = int(j in SIDE)
                    pool.wait_ge(e_y, j + 1)
                    if j != CHAINS[c][0]:
                        wait_added(pool, CHAINS[c][CHAINS[c].index(j) - 1])
                    nc.gpsimd.indirect_dma_start(out=plane, in_=ey[:, j % NY, :], in_offset=None,
                                                 out_offset=bass.IndirectOffsetOnAxis(ap=idx[:, 1, j:j + 1], axis=0),
                                                 compute_op=ALU.add).then_inc(d_plane[c], 16)
            wait_taken(pool, ("D1", NB - 1))
            for m in range(SIDE_POOL):
                x2 = xs[:, 2 * m:2 * m + 2, :]
                pool.wait_ge(d_fin[m], 32)
                link(nc.gpsimd.tensor_tensor(x2, x2, fin[m][:, 0, :, :], ALU.add))
                nc.gpsimd.tensor_tensor(x2, x2, fin[m][:, 1, :, :], ALU.add).then_inc(s_side, 1)
            for c in range(2):
                wait_added(pool, CHAINS[c][-1])

        @block.vector
        def _(dve):
            count = [0]

            def link(ins):
                count[0] += 1
                ins.then_inc(s_dve, 1)
                dve.wait_ge(s_dve, count[0])

            def note(ins):
                count[0] += 1
                ins.then_inc(s_dve, 1)

            def noted():
                dve.wait_ge(s_dve, count[0])

            V = nc.vector
            def stats(kind, b, i):
                if kind == 0 and i == 0:
                    dve.wait_ge(d_x[b], 16)
                V.bn_stats(stat[:, kind, i, :], xs[:, NT * b + i, :]).then_inc(s_stat, 1)

            def aggregate(kind, b):
                dve.wait_ge(s_stat, NT * NORM_AT[kind, b])
                for i in range(NT):
                    ins = V.bn_aggr(agg[:, kind, i, :], stat[:, kind, i, :])
                link(ins)
                if kind == 0 and b > 0 or kind == 1 and b > 0:
                    dve.wait_ge(s_xn, NORM_AT[kind, b - 1])
                V.tensor_scalar(rstd[:, kind, :], agg[:, kind, :, 1], EPS, None, ALU.add)
                V.tensor_scalar(shift[:, kind, :], agg[:, kind, :, 0], -1.0, None, ALU.mult).then_inc(s_var, 1)

            def logits(b, p):
                wait_product(dve, p)
                V.tensor_copy(lg[:, :, :], bank(p)[:, 0:P].rearrange("p (i e) -> p i e", i=NT)).then_inc(taken(p), 1)
                wait_taken(dve, p)
                note(V.tensor_reduce(gs[:, :, :], lg[:, :, :].rearrange("p i (g e) -> p (i g) e", g=G), AX.X, ALU.max))

            def compare(b):
                noted()
                mine = gs[:, :, :, None].broadcast_to([P, NT, G, G])
                other = gs[:, :, None, :].broadcast_to([P, NT, G, G])
                V.tensor_tensor(cmp[:, :, :, :], other, mine, ALU.is_gt)
                link(V.tensor_tensor(eq[:, :, :, :], other, mine, ALU.is_equal))
                note(V.tensor_tensor(eq[:, :, :, :], eq[:, :, :, :],
                                     tri[:, None, :, :].broadcast_to([P, NT, G, G]), ALU.mult))

            def mask(b):
                noted()
                link(V.tensor_tensor(cmp[:, :, :, :], cmp[:, :, :, :], eq[:, :, :, :], ALU.add))
                link(V.tensor_reduce(rank[:, :, :], cmp[:, :, :, :].rearrange("p i a c -> p (i a) c"), AX.X, ALU.add))
                note(V.tensor_scalar(rank[:, :, :], rank[:, :, :], TG - 0.5, None, ALU.is_lt))

            def shifted(b):
                noted()
                keep = rank[:, :, :].rearrange("p i g -> p (i g)")[:, :, None].broadcast_to([P, NT * G, EG])
                lgv = lg[:, :, :].rearrange("p i (g e) -> p (i g) e", g=G)
                link(V.tensor_tensor(lgv, lgv, keep, ALU.mult))
                link(V.tensor_reduce(exs[:, :, 0], lg[:, :, :], AX.X, ALU.max))
                V.tensor_tensor(lg[:, :, :], lg[:, :, :], exs[:, :, 0:1].broadcast_to([P, NT, E]),
                                ALU.subtract).then_inc(s_mask, 1)

            def best_probs(b):
                dve.wait_ge(s_ex, b + 1)
                V.tensor_reduce(exs[:, :, 1], ex[:, :, :], AX.X, ALU.add)
                for i in range(NT):
                    ins = V.max(top[:, i, :], ex[:, i, :])
                link(ins)
                V.reciprocal(exs[:, :, 2:3], exs[:, :, 1:2])
                note(V.memset(top[:, :, TOPK:8], -5.0))

            def mark(b):
                noted()
                for i in range(NT):
                    ins = V.match_replace(out=rep[:, i, :], in_to_replace=top[:, i, :], in_values=ex[:, i, :],
                                          imm_value=-1.0)
                note(ins)

            def choose(b):
                noted()
                link(V.tensor_scalar(exs[:, :, 3:4], exs[:, :, 2:3], SCALE_W, None, ALU.mult))
                V.tensor_scalar(sel[:, :, :], rep[:, :, :], 0.0, None, ALU.is_lt).then_inc(s_sel, 1)
                V.tensor_tensor(xr[:, :, H:XW], ex[:, :, :], exs[:, :, 3:4].broadcast_to([P, NT, E]),
                                ALU.mult).then_inc(s_row, 1)

            def best_half(b, n):
                r = (n + 1) // 2
                noted()
                if r == C // 8:
                    V.tensor_copy(cand[:, 0:C], best[:, :]).then_inc(s_best, 1)
                elif n % 2:
                    note(V.match_replace(out=cand[:, :], in_to_replace=best[:, 8 * r - 8:8 * r],
                                         in_values=cand[:, :], imm_value=0.0))
                else:
                    note(V.max(best[:, 8 * r:8 * r + 8], cand[:, :]))

            def next_keys(src, dst, r):
                if r:
                    link(V.match_replace(out=src, in_to_replace=dst[:, 8 * r - 8:8 * r], in_values=src,
                                         imm_value=0.0))
                return V.max(dst[:, 8 * r:8 * r + 8], src)

            def best_round(b, r):
                if b > 0 and r == 0:
                    dve.wait_ge(s_best, b)
                noted()
                note(next_keys(cand[:, :], best, r))
                if r == C // 8 - 1:
                    noted()
                    V.tensor_copy(cand[:, 0:C], best[:, :]).then_inc(s_best, 1)

            def consume(p):
                name, b = p
                if name in ("Q0", "Q1", "KV"):
                    c = ("Q0", "Q1", "KV").index(name)
                    n = 3 * b + c
                    m = P if c < 2 else NKV * HD
                    wait_product(dve, p)
                    if p == ("KV", 0):
                        dve.wait_ge(d_c0, 48)
                    if b > 0:
                        dve.wait_ge(s_lo[c], b)
                    V.stream_shuffle(qb[0:m, c, :], bank(p)[0:m, :], [i ^ 8 for i in range(32)])

            def consume_later(p):
                name, b = p
                if name in ("Q0", "Q1", "KV"):
                    c = ("Q0", "Q1", "KV").index(name)
                    m = P if c < 2 else NKV * HD
                    if c == 2:
                        dve.wait_ge(s_vt, b + 1)
                    V.tensor_tensor(qa[0:m, c, :], bank(p)[0:m, :], cos_s[0:m, :],
                                    ALU.mult).then_inc(taken(p), 1)
                if name in ("A0", "A2", "A4"):
                    c = int(name[1]) // 2
                    m = min(P, ISH - P * c)
                    dve.wait_ge(s_tanh, 3 * b + c + 1)
                    if c == 0 and b > 0:
                        wait_product(dve, ("D1", b - 1))
                    V.scalar_tensor_tensor(out=hs[0:m, c, :], in0=th[0:m, :], scalar=1.0, in1=bank(p)[0:m, :],
                                           op0=ALU.add, op1=ALU.mult).then_inc(taken(p), 1)

            def consume_small(p):
                name, b = p
                if name == "NT":
                    wait_product(dve, p)
                    if b >= 1:
                        wait_taken(dve, ("NT", b - 1))
                    if b % NKV == 0 and b > 0:
                        wait_product(dve, ("OT1", b // NKV - 1))
                    o = bank(p).rearrange("p (i h d) -> p i h d", i=NT, h=REP)
                    link(V.reciprocal(rec[:, :, :], o[:, :, :, HD]))
                    g = b % NKV
                    V.tensor_tensor(od[:, :, 64 * g:64 * g + 64].rearrange("p i (h d) -> p i h d", h=REP),
                                    o[:, :, :, 0:HD], rec[:, :, :, None].broadcast_to([P, NT, REP, HD]),
                                    ALU.mult).then_inc(taken(p), 1)
                if name == "MT":
                    wait_product(dve, p)
                    if b >= 2:
                        dve.wait_ge(d_mrow[b % 2], 48 * (b // 2))
                    row = mrow[:, b % 2, :, :]
                    link(V.tensor_scalar(row[:, 0, :], bank(p)[0:16, 0:P], -1.0, None, ALU.mult))
                    link(V.scalar_tensor_tensor(out=mr[:, :], in0=bank(p)[0:16, 0:P], scalar=-1.0, in1=row[:, 0, :],
                                                op0=ALU.mult, op1=ALU.subtract))
                    V.tensor_copy(row[:, 1, :], mr[:, :]).then_inc(taken(p), 1)
                    wait_taken(dve, p)
                    V.tensor_tensor(row[:, 2, :], mr[:, :], row[:, 1, :], ALU.subtract).then_inc(s_mrow, 1)
                if name in ("W0", "W1", "D0", "D1"):
                    i = NT * b + 2 * int(name[1])
                    wait_product(dve, p)
                    V.tensor_tensor(xs[:, i:i + 2, :], xs[:, i:i + 2, :],
                                    bank(p).rearrange("p (n h) -> p n h", n=2), ALU.add).then_inc(taken(p), 1)
                    wait_taken(dve, p)
                if name == "GT":
                    logits(b, p)
                if name in ("A1", "A3", "A5"):
                    c = int(name[1]) // 2
                    m = min(P, ISH - P * c)
                    wait_product(dve, p)
                    wait_taken(dve, (f"A{2 * c}", b))
                    V.scalar_tensor_tensor(out=hs[0:m, c, :], in0=hs[0:m, c, :], scalar=0.5, in1=bank(p)[0:m, :],
                                           op0=ALU.mult, op1=ALU.mult).then_inc(taken(p), 1)
                if name == "KP":
                    wait_product(dve, p)
                    keyp = bank(p)[:, 0:PAIRS]
                    V.tensor_scalar(idz[:, :], keyp, 0.0, pad[:, 0:1], ALU.is_equal, ALU.mult)
                    V.tensor_scalar(idf[:, :], keyp, -1.0, float(T), ALU.mult, ALU.add).then_inc(taken(p), 1)
                    wait_taken(dve, p)
                    link(V.tensor_tensor(idf[:, :], idf[:, :], idz[:, :], ALU.add))
                    V.tensor_copy(idx[:, 0, :], idf[:, :]).then_inc(s_idx, 1)
                    V.tensor_tensor(idx[:, 1, :], idf[:, :], pad[:, 1:1 + PAIRS], ALU.add).then_inc(s_idx, 1)
                if name == "ST":
                    wait_product(dve, p)
                    if b == 0:
                        dve.wait_ge(d_c1, 16 * 6)
                    V.tensor_tensor(cand[:, C:C + P], bank(p)[:, 0:P], keys[:, b, :], ALU.mult).then_inc(taken(p), 1)
                    wait_taken(dve, p)
                    for r in range(C // 8 if b == NB - 1 else 1):
                        best_round(b, r)

            V.memset(zero[:], 0.0).then_inc(s_zero, 1)
            for i in range(NT):
                stats(0, 0, i)
            V.memset(halfs[:], -0.5)
            aggregate(0, 0)
            for tile in (cand, best2):
                V.memset(tile[:], 0.0)
            V.memset(wsd_s[ISH - 2 * P:P, 2, :], 0.0)
            V.memset(hs[ISH - 2 * P:P, 2, :], 0.0)
            for n in range(NOWN):
                ins = V.memset(ew[n][:, EWG + H:EW], 0.0)
            ins.then_inc(s_const, 1)

            def rotate(c):
                m = P if c < 2 else NKV * HD
                wait_taken(dve, ((f"Q{c}", "KV")[c // 2], 0))
                link(V.tensor_tensor(qb[0:m, c, :], qb[0:m, c, :], sin_s[0:m, :], ALU.mult))
                V.tensor_tensor(qa[0:m, c, :], qa[0:m, c, :], qb[0:m, c, :], ALU.add).then_inc(s_roped[c], 1)

            def rest(c):
                m = P if c < 2 else NKV * HD
                dve.wait_ge(s_roped[c], 1)
                dve.wait_ge(s_hi[c], 1)
                V.tensor_tensor(qa[0:m, c, :], qa[0:m, c, :], part[0:m, 0, c, :], ALU.subtract).then_inc(s_res[c], 1)

            def low(c):
                m = P if c < 2 else NKV * HD
                dve.wait_ge(s_res[c], 1)
                dve.wait_ge(s_mid[c], 1)
                V.tensor_tensor(part[0:m, 2, c, :], qa[0:m, c, :], part[0:m, 1, c, :],
                                ALU.subtract).then_inc(s_lo[c], 1)

            consume(("KV", 0))
            consume_later(("KV", 0))
            rotate(2)
            consume(("Q0", 0))
            consume_later(("Q0", 0))
            rest(2)
            rotate(0)
            consume(("Q1", 0))
            consume_later(("Q1", 0))
            low(2)
            rest(0)
            low(0)
            for t in range(END + 1):
                if t < UNITS:
                    s, u = t // 16, t % 16
                    dve.wait_ge(s_p1, t + 1)
                    if u == 0 and s >= 2:
                        wait_product(dve, ("MT", s - 2))
                    V.tensor_reduce(mx[:, s % 2, u:u + 1], score[t % NA][:, 0, :], AX.X, ALU.max).then_inc(s_max, 1)
                for i in range(NT):
                    for kind, bb in norms_at(t - NSTATS[i]):
                        stats(kind, bb, i)
                for kind, bb in norms_at(t - NAGGR):
                    aggregate(kind, bb)
                for norm in norms_at(t - NAPPLY):
                    if norm == (1, NB - 1):
                        dve.wait_ge(s_rstd, NORM_AT[norm])
                        dve.wait_ge(d_scr, 16 * NB)
                        for i in (2, 3):
                            ins = V.tensor_scalar(xr[:, i, 0:H], xs[:, NT * (NB - 1) + i, :], agg[:, 1, i, 0:1],
                                                  rstd[:, 1, i:i + 1], ALU.subtract, ALU.mult)
                        ins.then_inc(s_xn, 1)
                if ("ST", NB - 1) in products_at(t - 6):
                    dve.wait_ge(d_merge, 16 * NT)
                    for r in range(C // 8):
                        ins = next_keys(merged[:, :], best2, r)
                        if r < C // 8 - 1:
                            link(ins)
                    ins.then_inc(s_tk, 1)
                for p in products_at(t - 1):
                    consume(p)
                    consume_small(p)
                for p in products_at(t - 2):
                    consume_later(p)
                for delay, piece in ((2, compare), (3, mask), (4, shifted), (7, best_probs),
                                     (8, mark), (9, choose)):
                    for p in products_at(t - delay):
                        if p[0] == "GT":
                            piece(p[1])
                for n in range(1, 2 * (C // 8)):
                    for p in products_at(t - 1 - n):
                        if p[0] == "ST" and p[1] < NB - 1:
                            best_half(p[1], n)
            def slot_weight(j):
                dve.wait_ge(d_gather[j], 16)
                V.tensor_tensor_reduce(out=wtmp[:, j, :], in0=xg[:, j % NXG, H:XW], in1=emask[:, j, :], scale=1.0,
                                       scalar=0.0, op0=ALU.mult, op1=ALU.add,
                                       accum_out=wslot[:, j:j + 1]).then_inc(s_ws, 1)
            def add_planes(m, turn):
                x2 = xs[:, 2 * m:2 * m + 2, :]
                if turn and m < SIDE_POOL:
                    wait_side(dve, m)
                dve.wait_ge(d_fin[m], 32 * (turn + 1))
                link(V.tensor_tensor(x2, x2, fin[m][:, 0, :, :], ALU.add))
                V.tensor_tensor(x2, x2, fin[m][:, 1, :, :], ALU.add).then_inc(s_fin, 1)

            for j in range(-1, PAIRS):
                n = j + 1
                if j >= 0:
                    dve.wait_ge(e_at, j + 1)
                    if j >= 2:
                        dve.wait_ge(e_dn, j - 1)
                    V.tensor_copy(eat[:, j % 2, 0, :], ps_o[:, 0, 0:P])
                    V.tensor_copy(eat[0:I - P, j % 2, 1, :], ps_o[0:I - P, 0, P:2 * P]).then_inc(e_atc, 1)
                if n < PAIRS:
                    dve.wait_ge(e_th, n + 1)
                    if n >= 2:
                        dve.wait_ge(e_at, n - 1)
                    a = egu[:, 2 + n % 2, :]
                    link(V.scalar_tensor_tensor(out=a, in0=egu[:, n % 2, :], scalar=1.0, in1=ps_s[:, n % 2, 0:I],
                                                op0=ALU.add, op1=ALU.mult))
                    V.scalar_tensor_tensor(out=a, in0=a, scalar=0.5, in1=ps_s[:, n % 2, I:2 * I],
                                           op0=ALU.mult, op1=ALU.mult).then_inc(e_act, 1)
                    slot_weight(n)
            for m in range(SIDE_POOL, CH):
                add_planes(m, 0)
            for m in MAIN:
                add_planes(m, 1)


def kernel(**inputs):
    import numpy as np
    import concourse.bacc as bacc
    from concourse.bass_utils import run_bass_kernel_spmd as run

    f = np.float32
    a = {k[3:]: np.ascontiguousarray(v) for k, v in inputs.items()}
    inv = (f(1.0) / f(10000.0) ** (np.arange(0, HD, 2, dtype=f) / f(HD))).astype(f)
    ang = np.arange(S, dtype=f)[None, :] * np.concatenate([inv, inv])[:, None]
    sign = np.where(np.arange(HD) < HD // 2, -1, 1).astype(f)[:, None]
    p, j = np.arange(P), np.arange(PAIRS)
    tile, lane = np.arange(P)[:, None, None] // E, np.arange(P)[None, None, :]
    token = S * np.arange(NB)[None, :, None] + P * tile + lane
    arrays = {
        "x": a["attn_x"].reshape(T, H),
        "wq": np.ascontiguousarray(a["attn_Wq"].T),
        "wkv": np.ascontiguousarray(np.concatenate([a["attn_Wk"], a["attn_Wv"]]).T),
        "wo": np.ascontiguousarray(a["attn_Wo"].T),
        "gate": np.ascontiguousarray(a["ffn_gate_w"].T),
        "wsgu": a["ffn_ws_gate_up"], "wsd": a["ffn_ws_down"],
        "wgu": a["ffn_w_gate_up"], "wd": a["ffn_w_down"],
        "cosr": np.tile(np.cos(ang), (P // HD, 1)).astype(f),
        "sinr": np.tile(np.sin(ang) * sign, (P // HD, 1)).astype(f),
        "ident_in": np.eye(P, dtype=f),
        "keys_in": (T - token).astype(f),
        "tri_in": np.ascontiguousarray(np.broadcast_to(np.tri(G, k=-1, dtype=f), (P, G, G))),
        "emask_in": (np.arange(E)[None, None, :] == (2 * j[None, :] + (p >= 64)[:, None])[:, :, None]).astype(f),
        "pad_in": np.concatenate([p[:, None], ROWS * ((p >= 64)[:, None] + 2 * np.isin(j, SIDE)[None, :])], 1).astype(f),
    }
    nc = bacc.Bacc("TRN2", target_bir_lowering=False, num_devices=1)
    args = [nc.dram_tensor(f"in_{k}", v.shape, mybir.dt.from_np(v.dtype), kind="ExternalInput").ap()
            for k, v in arrays.items()]
    out = nc.dram_tensor("out_0", (T, H), F32, kind="ExternalOutput").ap()
    moe_kernel(nc, *args, out)
    r = run(nc, [{f"in_{k}": v for k, v in arrays.items()}], core_ids=[0])
    return r.results[0]["out_0"].reshape(NB, S, H)
```
